# Optimizing a Trainium2 kernel written in Bass

```python
import numpy as np
import jax
import jax.numpy as jnp

def _softmax(x, axis=-1):
    return jax.nn.softmax(x, axis=axis)

def _gelu(x):
    return jax.nn.gelu(x, approximate=True)

def _silu(x):
    return jax.nn.silu(x)

def _sigmoid(x):
    return jax.nn.sigmoid(x)

def _layernorm(x, axis=-1, eps=1e-05):
    m = jnp.mean(x, axis=axis, keepdims=True)
    v = jnp.var(x, axis=axis, keepdims=True)
    return (x - m) / jnp.sqrt(v + eps)

def _scatter_add(tgt, idx, src, axis=0):
    return tgt.at[idx].add(src)

def _segment_sum(src, seg, n):
    return jax.ops.segment_sum(src, seg, n)
kernel_name = 'mk_rec_standalone_d1_rec_r8_67ad18'

def setup_inputs(seed: int=0):
    np.random.seed(seed)
    _w = jnp.asarray

    def _rec_inputs():
        import jax
        import jax.numpy as jnp
        _rk = jax.random.key(seed)
        r_coords = -0.00155981 + 0.998208 * jax.random.normal(jax.random.fold_in(_rk, 1), (2048, 10, 2), jnp.float32)
        r_region_idx = jnp.stack([jax.random.randint(jax.random.fold_in(jax.random.fold_in(_rk, 2), 0), (2048,), 0, 1250, jnp.int32), jax.random.randint(jax.random.fold_in(jax.random.fold_in(_rk, 2), 1), (2048,), 0, 1250, jnp.int32), jax.random.randint(jax.random.fold_in(jax.random.fold_in(_rk, 2), 2), (2048,), 0, 1250, jnp.int32), jax.random.randint(jax.random.fold_in(jax.random.fold_in(_rk, 2), 3), (2048,), 0, 1250, jnp.int32), jax.random.randint(jax.random.fold_in(jax.random.fold_in(_rk, 2), 4), (2048,), 0, 1250, jnp.int32), jax.random.randint(jax.random.fold_in(jax.random.fold_in(_rk, 2), 5), (2048,), 0, 1250, jnp.int32), jax.random.randint(jax.random.fold_in(jax.random.fold_in(_rk, 2), 6), (2048,), 0, 1250, jnp.int32), jax.random.randint(jax.random.fold_in(jax.random.fold_in(_rk, 2), 7), (2048,), 0, 9999, jnp.int32), jax.random.randint(jax.random.fold_in(jax.random.fold_in(_rk, 2), 8), (2048,), 0, 1250, jnp.int32), jax.random.randint(jax.random.fold_in(jax.random.fold_in(_rk, 2), 9), (2048,), 0, 1250, jnp.int32)], axis=1)
        r_poi_idx = jax.random.randint(jax.random.fold_in(_rk, 3), (2048, 10), 0, 64, jnp.int32)
        r_car_idx = jax.random.randint(jax.random.fold_in(_rk, 4), (2048,), 3, 499965, jnp.int32)
        r_week_idx = jax.random.randint(jax.random.fold_in(_rk, 5), (2048,), 0, 7, jnp.int32)
        r_time_idx = jax.random.randint(jax.random.fold_in(_rk, 6), (2048,), 0, 1440, jnp.int32)
        return (r_coords, r_region_idx, r_poi_idx, r_car_idx, r_week_idx, r_time_idx)
    r_coords, r_region_idx, r_poi_idx, r_car_idx, r_week_idx, r_time_idx = _rec_inputs()

    def _L0_rec_setup():
        import jax, jax.numpy as jnp
        import numpy as np
        from jax import lax
        B, T = (2048, 10)
        CAR, REG, POI, WEEK, TIME = (62500, 1250, 64, 7, 1440)
        H, LBL = (256, 512)

        def _lstm_layer(x, Wih, Whh, bih, bhh):
            Bx, Hh = (x.shape[0], Whh.shape[1])
            bias = bih + bhh

            def step(carry, xt):
                h, c = carry
                g = xt @ Wih.T + h @ Whh.T + bias
                i, f, gg, o = jnp.split(g, 4, axis=-1)
                c = jax.nn.sigmoid(f) * c + jax.nn.sigmoid(i) * jnp.tanh(gg)
                h = jax.nn.sigmoid(o) * jnp.tanh(c)
                return ((h, c), h)
            h0 = jnp.zeros((Bx, Hh), x.dtype)
            _, hs = lax.scan(step, (h0, h0), jnp.swapaxes(x, 0, 1))
            return jnp.swapaxes(hs, 0, 1)
        key = jax.random.key(seed)
        ks = jax.random.split(key, 32)
        p = lambda i, shp: jax.random.normal(ks[i], shp, jnp.float32) * 0.05
        d = {}
        d['region_idx'] = jax.random.randint(ks[0], (B, T), 0, REG)
        d['poi_idx'] = jax.random.randint(ks[1], (B, T), 0, POI)
        d['car_idx'] = jax.random.randint(ks[2], (B,), 0, CAR)
        d['week_idx'] = jax.random.randint(ks[3], (B,), 0, WEEK)
        d['time_idx'] = jax.random.randint(ks[4], (B,), 0, TIME)
        d['coords'] = jax.random.normal(ks[5], (B, T, 2), jnp.float32)
        d['region_tbl'] = p(6, (REG, 8))
        d['poi_tbl'] = p(7, (POI, 4))
        d['car_tbl'] = p(8, (CAR, 16))
        d['week_tbl'] = p(9, (WEEK, 3))
        d['time_tbl'] = p(10, (TIME, 8))
        d['W_rp'] = p(11, (12, 32))
        d['b_rp'] = p(12, (32,))
        d['W_co'] = p(13, (2, 8))
        d['b_co'] = p(14, (8,))
        d['conv_w'] = p(15, (3, 40, 32))
        d['conv_b'] = p(16, (32,))
        d['Wih0'] = p(17, (4 * H, 59))
        d['Whh0'] = p(18, (4 * H, H))
        d['bih0'] = p(19, (4 * H,))
        d['bhh0'] = p(20, (4 * H,))
        d['Wih1'] = p(21, (4 * H, H))
        d['Whh1'] = p(22, (4 * H, H))
        d['bih1'] = p(23, (4 * H,))
        d['bhh1'] = p(24, (4 * H,))
        d['W1'] = p(25, (H, 512))
        d['b1'] = p(26, (512,))
        d['W2'] = p(27, (512, 1024))
        d['b2'] = p(28, (1024,))
        d['W3'] = p(29, (1024, LBL))
        d['b3'] = p(30, (LBL,))
        return d
    _L0_rec_all = _L0_rec_setup()
    _L0_rec_in = {k: v for k, v in _L0_rec_all.items() if k in ('region_tbl', 'poi_tbl', 'car_tbl', 'week_tbl', 'time_tbl', 'W_rp', 'b_rp', 'W_co', 'b_co', 'conv_w', 'conv_b', 'Wih0', 'Whh0', 'bih0', 'bhh0', 'Wih1', 'Whh1', 'bih1', 'bhh1', 'W1', 'b1', 'W2', 'b2', 'W3', 'b3')}
    del _L0_rec_all
    return {'r_coords': r_coords, 'r_region_idx': r_region_idx, 'r_poi_idx': r_poi_idx, 'r_car_idx': r_car_idx, 'r_week_idx': r_week_idx, 'r_time_idx': r_time_idx, 'L0_rec_region_tbl': _L0_rec_in['region_tbl'], 'L0_rec_poi_tbl': _L0_rec_in['poi_tbl'], 'L0_rec_car_tbl': _L0_rec_in['car_tbl'], 'L0_rec_week_tbl': _L0_rec_in['week_tbl'], 'L0_rec_time_tbl': _L0_rec_in['time_tbl'], 'L0_rec_W_rp': _L0_rec_in['W_rp'], 'L0_rec_b_rp': _L0_rec_in['b_rp'], 'L0_rec_W_co': _L0_rec_in['W_co'], 'L0_rec_b_co': _L0_rec_in['b_co'], 'L0_rec_conv_w': _L0_rec_in['conv_w'], 'L0_rec_conv_b': _L0_rec_in['conv_b'], 'L0_rec_Wih0': _L0_rec_in['Wih0'], 'L0_rec_Whh0': _L0_rec_in['Whh0'], 'L0_rec_bih0': _L0_rec_in['bih0'], 'L0_rec_bhh0': _L0_rec_in['bhh0'], 'L0_rec_Wih1': _L0_rec_in['Wih1'], 'L0_rec_Whh1': _L0_rec_in['Whh1'], 'L0_rec_bih1': _L0_rec_in['bih1'], 'L0_rec_bhh1': _L0_rec_in['bhh1'], 'L0_rec_W1': _L0_rec_in['W1'], 'L0_rec_b1': _L0_rec_in['b1'], 'L0_rec_W2': _L0_rec_in['W2'], 'L0_rec_b2': _L0_rec_in['b2'], 'L0_rec_W3': _L0_rec_in['W3'], 'L0_rec_b3': _L0_rec_in['b3']}

def reference(r_coords, r_region_idx, r_poi_idx, r_car_idx, r_week_idx, r_time_idx, L0_rec_region_tbl, L0_rec_poi_tbl, L0_rec_car_tbl, L0_rec_week_tbl, L0_rec_time_tbl, L0_rec_W_rp, L0_rec_b_rp, L0_rec_W_co, L0_rec_b_co, L0_rec_conv_w, L0_rec_conv_b, L0_rec_Wih0, L0_rec_Whh0, L0_rec_bih0, L0_rec_bhh0, L0_rec_Wih1, L0_rec_Whh1, L0_rec_bih1, L0_rec_bhh1, L0_rec_W1, L0_rec_b1, L0_rec_W2, L0_rec_b2, L0_rec_W3, L0_rec_b3):
    import jax
    import jax.numpy as jnp

    def _L0_rec_ref(region_idx, poi_idx, car_idx, week_idx, time_idx, coords, region_tbl, poi_tbl, car_tbl, week_tbl, time_tbl, W_rp, b_rp, W_co, b_co, conv_w, conv_b, Wih0, Whh0, bih0, bhh0, Wih1, Whh1, bih1, bhh1, W1, b1, W2, b2, W3, b3):
        import jax, jax.numpy as jnp
        import numpy as np
        from jax import lax
        B, T = (2048, 10)
        CAR, REG, POI, WEEK, TIME = (62500, 1250, 64, 7, 1440)
        H, LBL = (256, 512)

        def _lstm_layer(x, Wih, Whh, bih, bhh):
            Bx, Hh = (x.shape[0], Whh.shape[1])
            bias = bih + bhh

            def step(carry, xt):
                h, c = carry
                g = xt @ Wih.T + h @ Whh.T + bias
                i, f, gg, o = jnp.split(g, 4, axis=-1)
                c = jax.nn.sigmoid(f) * c + jax.nn.sigmoid(i) * jnp.tanh(gg)
                h = jax.nn.sigmoid(o) * jnp.tanh(c)
                return ((h, c), h)
            h0 = jnp.zeros((Bx, Hh), x.dtype)
            _, hs = lax.scan(step, (h0, h0), jnp.swapaxes(x, 0, 1))
            return jnp.swapaxes(hs, 0, 1)
        rp = jnp.concatenate([region_tbl[region_idx], poi_tbl[poi_idx]], -1)
        nv = jnp.concatenate([rp @ W_rp + b_rp, coords @ W_co + b_co], -1)
        conv = jax.nn.elu(lax.conv_general_dilated(nv, conv_w, (1,), 'VALID', dimension_numbers=('NWC', 'WIO', 'NWC')) + conv_b)
        emb = jnp.tanh(jnp.concatenate([car_tbl[car_idx], week_tbl[week_idx], time_tbl[time_idx]], -1))
        x = jnp.concatenate([conv, jnp.broadcast_to(emb[:, None, :], conv.shape[:2] + (27,))], -1)
        h = _lstm_layer(x, Wih0, Whh0, bih0, bhh0)
        h = _lstm_layer(h, Wih1, Whh1, bih1, bhh1)
        last = h[:, -1, :]
        return ((last @ W1 + b1) @ W2 + b2) @ W3 + b3
    y = _L0_rec_ref(r_region_idx, r_poi_idx, r_car_idx, r_week_idx, r_time_idx, r_coords, L0_rec_region_tbl, L0_rec_poi_tbl, L0_rec_car_tbl, L0_rec_week_tbl, L0_rec_time_tbl, L0_rec_W_rp, L0_rec_b_rp, L0_rec_W_co, L0_rec_b_co, L0_rec_conv_w, L0_rec_conv_b, L0_rec_Wih0, L0_rec_Whh0, L0_rec_bih0, L0_rec_bhh0, L0_rec_Wih1, L0_rec_Whh1, L0_rec_bih1, L0_rec_bhh1, L0_rec_W1, L0_rec_b1, L0_rec_W2, L0_rec_b2, L0_rec_W3, L0_rec_b3)
    return y

_drawn_inputs = setup_inputs


def setup_inputs(seed=0):
    import zlib

    import numpy as np

    out = dict(_drawn_inputs(seed))
    spreads = {}
    factors = {'r_coords': 8.0,
     'L0_rec_region_tbl': 8.0,
     'L0_rec_poi_tbl': 8.0,
     'L0_rec_car_tbl': 3.518,
     'L0_rec_week_tbl': 5.048,
     'L0_rec_time_tbl': 3.667,
     'L0_rec_W_rp': 8.0,
     'L0_rec_b_rp': 5.659,
     'L0_rec_W_co': 8.0,
     'L0_rec_b_co': 5.197,
     'L0_rec_conv_w': 3.369,
     'L0_rec_conv_b': 4.659}
    for name, (base, spread) in spreads.items():
        noise = np.random.default_rng([zlib.crc32(name.encode()), seed]).standard_normal(out[name].shape)
        drawn = base * np.exp(spread * noise) if base else spread * noise
        out[name] = jnp.asarray(drawn.astype(out[name].dtype))
    for name, factor in factors.items():
        out[name] = (out[name] * factor).astype(out[name].dtype)
    return out
```

```python
from contextlib import ExitStack

import concourse.bass as bass
from concourse import mybir

F32 = mybir.dt.float32
F32R = mybir.dt.float32r
F16 = mybir.dt.float16
I32 = mybir.dt.int32
U32 = mybir.dt.uint32
ALU = mybir.AluOpType
ACT = mybir.ActivationFunctionType
AX = mybir.AxisListType

P = 128
NCOL = 512
GATE_I, GATE_F, GATE_G, GATE_O = range(4)
GATE_ORDER = (GATE_I, GATE_G, GATE_F, GATE_O)
HI, LO = 0, 1
DMA = 16

EXP_ONE = 1 << 23
EXP_MASK = 0x7F800000
EXP_LEAST = 121 * EXP_ONE
SCALE_FROM = (127 + 14 + 127) * EXP_ONE
UNSCALE_BY = 14 * EXP_ONE

ROW_CONV, ROW_EMB, ROW_LOW = 0, 32, 64


class Counts:

    def __init__(self, tile=0, half=0, rec=0, split=0, own=0):
        self.tile, self.half, self.rec, self.split, self.own = tile, half, rec, split, own

    def plus(self, o):
        return Counts(self.tile + o.tile, self.half + o.half, self.rec + o.rec, self.split + o.split,
                      self.own + o.own)

    def times(self, n):
        return Counts(self.tile * n, self.half * n, self.rec * n, self.split * n, self.own * n)


class Cell:

    def __init__(self, layer, first, last, read_slot, write_slot, x_slot, t, at, bank0):
        self.layer, self.first, self.last = layer, first, last
        self.read_slot, self.write_slot = read_slot, write_slot
        self.x_slot, self.t = x_slot, t
        self.tile, self.half, self.rec, self.split, self.own = at.tile, at.half, at.rec, at.split, at.own
        self.bank0 = bank0
        self.gates = [g for g in GATE_ORDER if not (first and g == GATE_F)]

    def bank(self, j, g):
        return (self.bank0 + self.place(j, g)) % 4

    def place(self, j, g):
        return j * len(self.gates) + self.gates.index(g)


def cell_size(first, last):
    return Counts(6 if first else 8, 2, 0 if first else 2, 0 if last else 2)


def stages(eng, nbatch, steps):
    snap = eng.snap
    plain, opening, closing = cell_size(False, False), cell_size(True, False), cell_size(False, True)
    per_step = plain.plus(plain).plus(Counts(own=2))
    per_batch = opening.plus(opening).plus(plain.times(2 * steps - 3)).plus(closing).plus(Counts(own=2 * steps))
    assert per_batch.tile % 4 == 0 and per_step.tile % 4 == 0

    def snapped(c):
        return Counts(snap(c.tile), snap(c.half), snap(c.rec), snap(c.split), snap(c.own))

    def cell(layer, t, n, x_slot, before, offset, own):
        at = before.plus(offset).plus(Counts(own=own))
        return Cell(layer, t == 0, layer == 1 and t == steps - 1, (t + 1) % 2, t % 2, x_slot, t, at,
                    before.tile % 4)

    def body(n, offset, following):
        x_slot = n % 2 if isinstance(n, int) else snap(n % 2)
        before = opening
        yield "cell", cell(0, 1, n, x_slot, before, offset, 2)
        before = before.plus(plain)
        yield "cell", cell(1, 0, n, x_slot, before, offset, 0)
        before = before.plus(opening)
        with eng.Fori(0, steps - 3) as u:
            t = snap(u + 2)
            even, odd = snap(t % 2), snap((u + 1) % 2)
            inner = snapped(offset.plus(per_step.times(u)))
            at = before.plus(inner).plus(Counts(own=4))
            yield "cell", Cell(0, False, False, odd, even, x_slot, t, at, before.tile % 4)
            before_upper = before.plus(plain)
            at = before_upper.plus(inner).plus(Counts(own=2))
            yield "cell", Cell(1, False, False, even, odd, x_slot, t, at, before_upper.tile % 4)
        before = before.plus(plain.times(2 * (steps - 3)))
        if following:
            yield "transpose", n + 1
        yield "cell", cell(0, steps - 1, n, x_slot, before, offset, 2 * steps - 2)
        before = before.plus(plain)
        if following:
            yield "conv", n + 1
        yield "cell", cell(1, steps - 2, n, x_slot, before, offset, 2 * steps - 4)
        before = before.plus(plain)
        if following:
            next_slot = (n + 1) % 2 if isinstance(n, int) else snap((n + 1) % 2)
            following_cell = cell(0, 0, n, next_slot, before, offset, 2 * steps)
            following_cell.batch = n + 1
            yield "cell", following_cell
            before = before.plus(opening)
        yield "cell", cell(1, steps - 1, n, x_slot, before, offset, 2 * steps - 2)
        yield "head", n

    yield "transpose", 0
    yield "conv", 0
    first = cell(0, 0, 0, 0, Counts(), Counts(), 0)
    first.batch = 0
    yield "cell", first
    with eng.Fori(0, nbatch - 1) as n:
        yield from body(n, snapped(per_batch.times(n)), True)
    yield from body(nbatch - 1, per_batch.times(nbatch - 1), False)


def build(nc, d):
    B, T, _ = d["r_coords"].shape
    REG, D_REG = d["region_tbl"].shape
    POI, D_POI = d["poi_tbl"].shape
    CAR, D_CAR = d["car_tbl"].shape
    WEEK, D_WEEK = d["week_tbl"].shape
    TIME, D_TIME = d["time_tbl"].shape
    D_RP = d["W_rp"].shape[1]
    D_CO = d["W_co"].shape[1]
    TAPS, D_NV, D_CONV = d["conv_w"].shape
    D_FEAT = D_REG + D_POI + 2
    D_EMB = D_CAR + D_WEEK + D_TIME
    D_X = D_CONV + D_EMB
    GATES, H = d["Whh0"].shape
    HK = H // P
    M = GATES // P
    D1, D2, D3 = d["W1"].shape[1], d["W2"].shape[1], d["W3"].shape[1]
    STEPS = T - TAPS + 1
    NB = B // NCOL
    GR = NCOL // P
    TT = P // D_CONV
    CH = STEPS // TT
    WIN = (TT + TAPS - 1)
    KF = WIN * D_FEAT
    assert HK == 2 and M == 8 and CH == 2 and D_RP + D_CO == D_NV and ROW_EMB + D_EMB <= ROW_LOW

    with ExitStack() as ctx:
        def sb(name, shape, dt, stack=ctx):
            return stack.enter_context(nc.sbuf_tensor(name, shape, dt))

        def sem(name):
            return ctx.enter_context(nc.semaphore(name))

        idx_raw = {"region": sb("region_raw", [P, NB * GR, T], I32), "poi": sb("poi_raw", [P, NB * GR, T], I32),
                   "car": sb("car_raw", [P, NB * GR, 1], I32), "week": sb("week_raw", [P, NB * GR, 1], I32),
                   "time": sb("time_raw", [P, NB * GR, 1], I32)}
        idx_wrap = sb("idx_wrap", [P, NB * GR, T], F32)
        idx = {k: sb(f"{k}_idx", list(v.shape), I32) for k, v in idx_raw.items()}
        coords = sb("coords", [P, NB * GR, T * 2], F32)
        feat = sb("feat", [P, GR, T, D_FEAT], F32)
        emb = sb("emb", [P, GR, ROW_LOW], F32)
        feat_t = sb("feat_t", [KF, CH, NCOL], F32)
        relu_part = sb("relu_part", [P, CH, NCOL], F32)
        neg_part = sb("neg_part", [P, CH, NCOL], F32)
        tanh_part = sb("tanh_part", [P, CH, NCOL], F32)
        conv_hi = sb("conv_hi", [P, CH, NCOL], F32R)
        conv_lo = sb("conv_lo", [P, CH, NCOL], F32R)
        emb_tanh = sb("emb_tanh", [ROW_LOW, NCOL], F32)
        emb_hi = sb("emb_hi", [ROW_LOW, NCOL], F32R)
        emb_lo = sb("emb_lo", [ROW_LOW, NCOL], F32R)
        x_in = sb("x_in", [P, 2, STEPS, NCOL], F32R)
        wx = sb("wx", [P, 2, GATES], F32R)
        wh = sb("wh", [P, 3, 2, HK, GATES], F16)
        w_head = sb("w_head", [P, HK, D3], F32)
        b_head = sb("b_head", [P, D3], F32)
        conv_band = sb("conv_band", [KF, P], F32)
        conv_bias = sb("conv_bias", [P, 1], F32)
        gate_bias = sb("gate_bias", [P, 2, M], F32)
        unscale = sb("unscale", [P, 2, M], F32)
        ident = sb("ident", [P, P], F32)
        before_first = sb("before_first", [P, 2], F32)
        ident16 = sb("ident16", [P, P], F16)

        with ExitStack() as setup:
            w_nat = sb("w_nat", [P, 3, M, H], F32, setup)
            wx_nat = sb("wx_nat", [P, M, P], F32, setup)
            w_part = sb("w_part", [P, 2, M, H], F16, setup)
            w1_nat = sb("w1_nat", [P, HK, D1], F32, setup)
            w1_t = sb("w1_t", [P, D1 // P, H + 1], F32, setup)
            w2 = sb("w2", [P, D1 // P, D2], F32, setup)
            w3 = sb("w3", [P, D2 // P, D3], F32, setup)
            w12_t = sb("w12_t", [P, D2 // P, H + 1], F32, setup)
            b2_col = sb("b2_col", [P, D2 // P], F32, setup)
            b3_row = sb("b3_row", [P, D3], F32, setup)
            bias_in = sb("bias_in", [P, 2, 2, M], F32, setup)
            row_max = sb("row_max", [P, 3, M], F32, setup)
            exp_bits = sb("exp_bits", [P, 2, M], I32, setup)
            row_scale = sb("row_scale", [P, 2, M], F32, setup)
            PAD = (WIN - 1) * D_FEAT
            proj_t = sb("proj_t", [D_NV, PAD + D_FEAT + PAD], F32, setup)
            conv_w = sb("conv_w", [D_NV, TAPS, D_CONV], F32, setup)
            proj_bias = sb("proj_bias", [D_NV, 1], F32, setup)
            conv_b = sb("conv_b", [P, 1], F32, setup)

        gates = sb("gates", [P, 2, HK, 4, NCOL], F32)
        ig = sb("ig", [P, 2, NCOL], F32)
        cell_c = sb("cell_c", [P, 2, HK, NCOL], F32)
        tanh_c = sb("tanh_c", [P, 2, HK, NCOL], F32)
        h_full = sb("h_full", [P, 2, NCOL], F32)
        h_part = sb("h_part", [P, 2, 2, 2, HK, NCOL], F16)
        h_last = sb("h_last", [P, HK, NCOL], F32)
        y = sb("y", [P, GR, D3], F32)

        acc = ctx.enter_context(nc.psum_tensor("acc", [P, 4, NCOL], F32))
        aux = ctx.enter_context(nc.psum_tensor("aux", [P, 4, NCOL], F32))

        idx_in = {k: sem(f"{k}_in") for k in idx_raw}
        coords_in = sem("coords_in")
        w_in = [sem(f"w_in{i}") for i in range(3)]
        wx_in = sem("wx_in")
        bias_loaded = sem("bias_loaded")
        proj_in = sem("proj_in")
        w1_in, w2_in, w3_in = sem("w1_in"), sem("w2_in"), sem("w3_in")
        gathered = sem("gathered")
        zeroed = sem("zeroed")
        ident_zero, ident_ready, ident16_ready = sem("ident_zero"), sem("ident_ready"), sem("ident16_ready")
        idx_step, idx_ready = sem("idx_step"), sem("idx_ready")
        coords_put = sem("coords_put")
        prep = sem("prep")
        scaled = sem("scaled")
        part_hi, part_lo = sem("part_hi"), sem("part_lo")
        part_turned = sem("part_turned")
        part_put = sem("part_put")
        band_acc, band_put = sem("band_acc"), sem("band_put")
        wx_turned, wx_hi_put, wx_lo_put = sem("wx_turned"), sem("wx_hi_put"), sem("wx_lo_put")
        w1_turned, w1_put = sem("w1_turned"), sem("w1_put")
        w12_acc, w12_put = sem("w12_acc"), sem("w12_put")
        head_acc, head_put = sem("head_acc"), sem("head_put")
        feat_turned, feat_put = sem("feat_turned"), sem("feat_put")
        emb_turned, emb_act = sem("emb_turned"), sem("emb_act")
        emb_hi_put, emb_lo_put = sem("emb_hi_put"), sem("emb_lo_put")
        conv_acc = sem("conv_acc")
        relu_done, neg_done, tanh_done = sem("relu_done"), sem("neg_done"), sem("tanh_done")
        elu_step, conv_hi_put, conv_lo_put = sem("elu_step"), sem("conv_hi_put"), sem("conv_lo_put")
        x_put = sem("x_put")
        gate_acc, gate_act = sem("gate_acc"), sem("gate_act")
        ig_done, fc_done, c_done, tanh_c_done = sem("ig_done"), sem("fc_done"), sem("c_done"), sem("tanh_c_done")
        h_full_done, h_hi_done = sem("h_full_done"), sem("h_hi_done")
        h_done = [sem("h0_done"), sem("h1_done")]
        y_acc, y_put, y_out = sem("y_acc"), sem("y_put"), sem("y_out")

        PER_GATHER = (2 * GR * T + 3 * GR) * DMA
        PER_X = (2 * STEPS + 2) * DMA
        ahead = 2
        tables = {"region": d["region_tbl"], "poi": d["poi_tbl"], "car": d["car_tbl"],
                  "week": d["week_tbl"], "time": d["time_tbl"]}

        block = ctx.enter_context(nc.Block())

        @block.sync
        def _(sp):
            for k in ("region", "poi"):
                sp.dma_start(idx_raw[k][:, :, :].rearrange("p (n g) t -> p n g t", g=GR),
                             d[f"r_{k}_idx"].rearrange("(n p g) t -> p n g t", p=P, g=GR)).then_inc(idx_in[k], DMA)
            for k in ("car", "week", "time"):
                sp.dma_start(idx_raw[k][:, :, 0].rearrange("p (n g) -> p n g", g=GR),
                             d[f"r_{k}_idx"].rearrange("(n p g) -> p n g", p=P, g=GR)).then_inc(idx_in[k], DMA)
            sp.dma_start(coords[:, :, :].rearrange("p (n g) x -> p n g x", g=GR),
                         d["r_coords"].rearrange("(n p g) t c -> p n g (t c)", p=P, g=GR)).then_inc(coords_in, DMA)
            sp.wait_ge(zeroed, 3)
            sp.dma_start(proj_t[0:D_RP, PAD:PAD + D_REG + D_POI], d["W_rp"].rearrange("i o -> o i"), allow_slow_non_contiguous=True
                         ).then_inc(proj_in, DMA)
            sp.dma_start(proj_t[D_RP:D_NV, PAD + D_REG + D_POI:PAD + D_FEAT], d["W_co"].rearrange("i o -> o i"), allow_slow_non_contiguous=True
                         ).then_inc(proj_in, DMA)
            sp.dma_start(conv_w[:, :, :], d["conv_w"].rearrange("k i o -> i k o")).then_inc(proj_in, DMA)
            sp.dma_start(proj_bias[0:D_RP, 0], d["b_rp"], allow_slow_non_contiguous=True
                             ).then_inc(proj_in, DMA)
            sp.dma_start(proj_bias[D_RP:D_NV, 0], d["b_co"], allow_slow_non_contiguous=True
                             ).then_inc(proj_in, DMA)
            for s in range(TT):
                sp.dma_start(conv_b[s * D_CONV:(s + 1) * D_CONV, 0], d["conv_b"], allow_slow_non_contiguous=True
                             ).then_inc(proj_in, DMA)
            for row in (ROW_CONV, ROW_LOW):
                sp.dma_start(wx_nat[:, :, row:row + D_X], d["Wih0"].rearrange("(m p) k -> p m k", p=P)
                             ).then_inc(wx_in, DMA)
            for i, k in enumerate(("Whh0", "Wih1", "Whh1")):
                sp.dma_start(w_nat[:, i, :, :], d[k].rearrange("(m p) k -> p m k", p=P)).then_inc(w_in[i], DMA)
            for layer in range(2):
                for s, k in enumerate(("bih", "bhh")):
                    sp.dma_start(bias_in[:, layer, s, :], d[f"{k}{layer}"].rearrange("(m p) -> p m", p=P), allow_slow_non_contiguous=True
                             ).then_inc(bias_loaded, DMA)
            sp.dma_start(w1_nat[:, :, :], d["W1"].rearrange("(a p) n -> p a n", p=P)).then_inc(w1_in, DMA)
            sp.dma_start(w1_t[:, :, H], d["b1"].rearrange("(k p) -> p k", p=P), allow_slow_non_contiguous=True
                             ).then_inc(w1_in, DMA)
            sp.dma_start(w2[:, :, :], d["W2"].rearrange("(k p) n -> p k n", p=P)).then_inc(w2_in, DMA)
            sp.dma_start(b2_col[:, :], d["b2"].rearrange("(k p) -> p k", p=P), allow_slow_non_contiguous=True
                             ).then_inc(w2_in, DMA)
            sp.dma_start(w3[:, :, :], d["W3"].rearrange("(k p) n -> p k n", p=P)).then_inc(w3_in, DMA)
            sp.dma_start(b3_row[:, :], d["b3"].rearrange("(a n) -> a n", a=1).partition_broadcast(P)[:, 0, :]
                         ).then_inc(w3_in, DMA)

            out_rows = d["out"].rearrange("(n p g) o -> p n g o", p=P, g=GR)
            for kind, s in stages(sp, NB, STEPS):
                if kind == "transpose":
                    slot = s % 2
                    for part, tile, put in ((0, emb_hi, emb_hi_put), (ROW_LOW, emb_lo, emb_lo_put)):
                        sp.wait_ge(put, s + 1)
                        src = tile[ROW_EMB:ROW_LOW, :].bitcast(F32).unsqueeze(1).to_broadcast([ROW_LOW - ROW_EMB, STEPS, NCOL])
                        sp.dma_start(x_in[part + ROW_EMB:part + ROW_LOW, slot, :, :].bitcast(F32), src).then_inc(x_put, DMA)
                elif kind == "conv":
                    slot = s % 2
                    for c in range(CH):
                        for part, tile, put in ((0, conv_hi, conv_hi_put), (ROW_LOW, conv_lo, conv_lo_put)):
                            if c == 0:
                                sp.wait_ge(put, s + 1)
                            for k in range(TT):
                                sp.dma_start(x_in[part:part + D_CONV, slot, c * TT + k, :].bitcast(F32),
                                             tile[k * D_CONV:(k + 1) * D_CONV, c, :].bitcast(F32)
                                             ).then_inc(x_put, DMA)
                elif kind == "head":
                    for g in range(GR):
                        sp.wait_ge(y_put, s * GR + g + 1)
                        sp.dma_start(out_rows[:, s, g, :], y[:, g, :]).then_inc(y_out, DMA)
            sp.wait_ge(y_out, NB * GR * DMA)

        @block.gpsimd
        def _(pool):
            nc.gpsimd.memset(emb[:, :, :], 0.0).then_inc(zeroed, 1)
            nc.gpsimd.memset(wx_nat[:, :, :], 0.0).then_inc(zeroed, 1)
            nc.gpsimd.memset(proj_t[:, :], 0.0).then_inc(zeroed, 1)
            nc.gpsimd.memset(ident[:, :], 0.0).then_inc(ident_zero, 1)
            pool.wait_ge(ident_zero, 1)
            nc.gpsimd.affine_select(out=ident[:, :], in_=ident[:, :], compare_op=ALU.not_equal, fill=1.0,
                                    base=0, pattern=[[-1, P]], channel_multiplier=1).then_inc(ident_ready, 1)
            pool.wait_ge(zeroed, 3)
            for n in range(NB):
                if n:
                    pool.wait_ge(feat_turned, n)
                    pool.wait_ge(emb_turned, n)
                else:
                    pool.wait_ge(idx_ready, 5)
                    pool.wait_ge(coords_in, DMA)
                nc.gpsimd.tensor_copy(feat[:, :, :, D_REG + D_POI:D_FEAT],
                                      coords[:, n * GR:(n + 1) * GR, :].rearrange("p g (t c) -> p g t c", c=2)
                                      ).then_inc(coords_put, 1)

                def gather(k, out, g, t):
                    pool.indirect_dma_start(out, None, tables[k],
                                            bass.IndirectOffsetOnAxis(ap=idx[k][:, n * GR + g, t:t + 1], axis=0)
                                            ).then_inc(gathered, DMA)

                for g in range(GR):
                    for t in range(T):
                        gather("region", feat[:, g, t, 0:D_REG], g, t)
                        gather("poi", feat[:, g, t, D_REG:D_REG + D_POI], g, t)
                    gather("car", emb[:, g, ROW_EMB:ROW_EMB + D_CAR], g, 0)
                    gather("week", emb[:, g, ROW_EMB + D_CAR:ROW_EMB + D_CAR + D_WEEK], g, 0)
                    gather("time", emb[:, g, ROW_EMB + D_CAR + D_WEEK:ROW_EMB + D_EMB], g, 0)
                pool.wait_ge(gathered, PER_GATHER * (n + 1))

        @block.scalar
        def _(act):
            for i in range(3):
                act.wait_ge(scaled, i + 1)
                if i:
                    act.wait_ge(part_turned, 2 * HK * i)
                nc.scalar.copy(w_part[:, HI, :, :], w_nat[:, i, :, :]).then_inc(part_hi, 1)
                for part in (HI, LO):
                    for k in range(HK):
                        b = 2 * HK * i + HK * part + k
                        act.wait_ge(part_turned, b + 1)
                        nc.scalar.copy(wh[:, i, part, k, :], aux[:, b % 4, :].bitcast(F16)).then_inc(part_put, 1)
            act.wait_ge(w2_in, 2 * DMA)
            for m in range(D2 // P):
                act.wait_ge(w12_acc, m + 1)
                nc.scalar.copy(w12_t[:, m, 0:H], acc[:, 2 + m % 2, 0:H]).then_inc(w12_put, 1)
                nc.scalar.activation(w12_t[:, m, H:H + 1], acc[:, 2 + m % 2, H:H + 1], ACT.Identity,
                                     bias=b2_col[:, m:m + 1]).then_inc(w12_put, 1)
            for k in range(HK):
                act.wait_ge(head_acc, k + 1)
                nc.scalar.copy(w_head[:, k, :], acc[:, k, :]).then_inc(head_put, 1)

            act.wait_ge(prep, 9)
            for kind, s in stages(act, NB, STEPS):
                if kind == "transpose":
                    act.wait_ge(emb_turned, s + 1)
                    if not (isinstance(s, int) and s == 0):
                        act.wait_ge(emb_lo_put, s)
                    nc.scalar.activation(emb_tanh[:, :], aux[0:ROW_LOW, 2, :], ACT.Tanh).then_inc(emb_act, 1)
                elif kind == "conv":
                    act.wait_ge(conv_acc, s + 1)
                    act.wait_ge(band_put, 2)
                    if not (isinstance(s, int) and s == 0):
                        act.wait_ge(conv_lo_put, s)
                    nc.scalar.activation(relu_part[:, :, :], aux[:, 2:4, :], ACT.Relu,
                                         bias=conv_bias[:, 0:1]).then_inc(relu_done, 1)
                    act.wait_ge(neg_done, s + 1)
                    nc.scalar.activation(tanh_part[:, :, :], neg_part[:, :, :], ACT.Tanh,
                                         scale=0.5).then_inc(tanh_done, 1)
                elif kind == "cell":
                    k = s.tile
                    for j in range(HK):
                        act.wait_ge(h_done[s.layer], ahead + s.own + j - 1)
                        for g in s.gates:
                            act.wait_ge(gate_acc, k + 1)
                            m = g * HK + j
                            nc.scalar.activation(gates[:, s.layer, j, g, :], acc[:, s.bank(j, g), :],
                                                 ACT.Tanh if g == GATE_G else ACT.Sigmoid,
                                                 bias=gate_bias[:, s.layer, m:m + 1],
                                                 scale=unscale[:, s.layer, m:m + 1]).then_inc(gate_act, 1)
                            k = k + 1
                        act.wait_ge(c_done, s.half + j + 1)
                        nc.scalar.activation(tanh_c[:, s.layer, j, :], cell_c[:, s.layer, j, :], ACT.Tanh
                                             ).then_inc(tanh_c_done, 1)

        @block.vector
        def _(dve):
            for layer in range(2):
                nc.vector.memset(before_first[:, layer:layer + 1], 0.0).then_inc(h_done[layer], ahead)
            steps = 0
            for k, rows in (("region", REG), ("poi", POI), ("car", CAR), ("week", WEEK), ("time", TIME)):
                dve.wait_ge(idx_in[k], DMA)
                raw = idx_raw[k]
                wrap = idx_wrap[:, :, 0:raw.shape[2]]
                nc.vector.tensor_scalar(wrap, raw[:, :, :], 0.0, float(rows), ALU.is_lt, ALU.mult
                                        ).then_inc(idx_step, 1)
                dve.wait_ge(idx_step, steps + 1)
                nc.vector.tensor_tensor(wrap, wrap, raw[:, :, :], ALU.add).then_inc(idx_step, 1)
                dve.wait_ge(idx_step, steps + 2)
                nc.vector.tensor_scalar(idx[k][:, :, :], wrap, 0.0, float(rows - 1), ALU.max, ALU.min
                                        ).then_inc(idx_ready, 1)
                steps += 2
                dve.wait_ge(idx_ready, steps // 2)
            dve.wait_ge(ident_ready, 1)
            nc.vector.tensor_copy(ident16[:, :], ident[:, :]).then_inc(ident16_ready, 1)

            dve.wait_ge(band_acc, 2)
            nc.vector.tensor_copy(conv_band[:, :], aux[0:KF, 0, 0:P]).then_inc(band_put, 1)
            nc.vector.tensor_tensor(conv_bias[:, :], aux[:, 1, 0:1], conv_b[:, :], ALU.add).then_inc(band_put, 1)

            for i in range(3):
                dve.wait_ge(w_in[i], DMA)
                nc.vector.tensor_reduce(row_max[:, i, :], w_nat[:, i, :, :], AX.X, ALU.max,
                                        apply_absolute_value=True).then_inc(prep, 1)
            dve.wait_ge(prep, 3)
            nc.vector.tensor_tensor(row_max[:, 1, :], row_max[:, 1, :], row_max[:, 2, :], ALU.max).then_inc(prep, 1)
            dve.wait_ge(prep, 4)
            nc.vector.tensor_scalar(exp_bits[:, :, :], row_max[:, 0:2, :].bitcast(I32), EXP_MASK, None,
                                    ALU.bitwise_and).then_inc(prep, 1)
            dve.wait_ge(prep, 5)
            nc.vector.tensor_scalar(exp_bits[:, :, :], exp_bits[:, :, :], float(EXP_LEAST), None, ALU.max
                                    ).then_inc(prep, 1)
            dve.wait_ge(prep, 6)
            nc.vector.tensor_scalar(row_scale[:, :, :].bitcast(I32), exp_bits[:, :, :], -1.0, float(SCALE_FROM),
                                    ALU.mult, ALU.add).then_inc(prep, 1)
            nc.vector.tensor_scalar(unscale[:, :, :].bitcast(I32), exp_bits[:, :, :], float(-UNSCALE_BY), None,
                                    ALU.add).then_inc(prep, 1)
            dve.wait_ge(bias_loaded, 4 * DMA)
            nc.vector.tensor_tensor(gate_bias[:, :, :], bias_in[:, :, 0, :], bias_in[:, :, 1, :], ALU.add
                                    ).then_inc(prep, 1)
            dve.wait_ge(prep, 9)

            dve.wait_ge(wx_in, 2 * DMA)
            nc.vector.tensor_tensor(wx_nat[:, :, :], wx_nat[:, :, :],
                                    row_scale[:, 0, :].unsqueeze(2).to_broadcast([P, M, P]), ALU.mult
                                    ).then_inc(prep, 1)

            def scale_weights(i):
                layer = 0 if i == 0 else 1
                nc.vector.tensor_tensor(w_nat[:, i, :, :], w_nat[:, i, :, :],
                                        row_scale[:, layer, :].unsqueeze(2).to_broadcast([P, M, H]), ALU.mult
                                        ).then_inc(scaled, 1)

            def low_parts(i):
                dve.wait_ge(part_hi, i + 1)
                nc.vector.tensor_tensor(w_part[:, LO, :, :], w_nat[:, i, :, :], w_part[:, HI, :, :], ALU.subtract
                                        ).then_inc(part_lo, 1)

            scale_weights(0)
            for b in range(2):
                dve.wait_ge(wx_turned, b + 1)
                cols = slice(b * NCOL, (b + 1) * NCOL)
                nc.vector.tensor_copy(wx[:, HI, cols], acc[:, b, :]).then_inc(wx_hi_put, 1)
                dve.wait_ge(wx_hi_put, b + 1)
                nc.vector.tensor_tensor(wx[:, LO, cols], acc[:, b, :], wx[:, HI, cols].bitcast(F32), ALU.subtract
                                        ).then_inc(wx_lo_put, 1)
            low_parts(0)
            scale_weights(1)
            scale_weights(2)
            low_parts(1)
            low_parts(2)
            for b in range(2):
                dve.wait_ge(w1_turned, b + 1)
                nc.vector.tensor_copy(w1_t[:, 2 * b:2 * b + 2, 0:H],
                                      acc[:, b, :].rearrange("p (k a) -> p k a", k=2)).then_inc(w1_put, 1)
            dve.wait_ge(head_acc, HK + 1)
            dve.wait_ge(w3_in, 2 * DMA)
            nc.vector.tensor_tensor(b_head[:, :], aux[:, 0, :], b3_row[:, :], ALU.add).then_inc(head_put, 1)

            for kind, s in stages(dve, NB, STEPS):
                start = isinstance(s, int) and s == 0
                if kind == "transpose":
                    dve.wait_ge(feat_turned, s + 1)
                    nc.vector.tensor_copy(feat_t[:, :, :], aux[0:KF, 0:2, :]).then_inc(feat_put, 1)
                    dve.wait_ge(emb_act, s + 1)
                    if not start:
                        dve.wait_ge(x_put, s * PER_X)
                    nc.vector.tensor_copy(emb_hi[:, :], emb_tanh[:, :]).then_inc(emb_hi_put, 1)
                    dve.wait_ge(emb_hi_put, s + 1)
                    nc.vector.tensor_tensor(emb_lo[:, :], emb_tanh[:, :], emb_hi[:, :].bitcast(F32), ALU.subtract
                                            ).then_inc(emb_lo_put, 1)
                elif kind == "conv":
                    dve.wait_ge(relu_done, s + 1)
                    nc.vector.tensor_scalar(neg_part[:, :, :], aux[:, 2:4, :], conv_bias[:, 0:1], 0.0,
                                            ALU.add, ALU.min).then_inc(neg_done, 1)
                    dve.wait_ge(tanh_done, s + 1)
                    nc.vector.tensor_scalar(neg_part[:, :, :], tanh_part[:, :, :], -1.0, 1.0, ALU.mult, ALU.add
                                            ).then_inc(elu_step, 1)
                    dve.wait_ge(elu_step, 4 * s + 1)
                    nc.vector.reciprocal(neg_part[:, :, :], neg_part[:, :, :]).then_inc(elu_step, 1)
                    dve.wait_ge(elu_step, 4 * s + 2)
                    nc.vector.scalar_tensor_tensor(neg_part[:, :, :], tanh_part[:, :, :], 2.0, neg_part[:, :, :],
                                                   ALU.mult, ALU.mult).then_inc(elu_step, 1)
                    dve.wait_ge(elu_step, 4 * s + 3)
                    nc.vector.tensor_tensor(relu_part[:, :, :], relu_part[:, :, :], neg_part[:, :, :], ALU.add
                                            ).then_inc(elu_step, 1)
                    dve.wait_ge(elu_step, 4 * s + 4)
                    nc.vector.tensor_copy(conv_hi[:, :, :], relu_part[:, :, :]).then_inc(conv_hi_put, 1)
                    dve.wait_ge(conv_hi_put, s + 1)
                    nc.vector.tensor_tensor(conv_lo[:, :, :], relu_part[:, :, :], conv_hi[:, :, :].bitcast(F32),
                                            ALU.subtract).then_inc(conv_lo_put, 1)
                elif kind == "cell":
                    tile = s.tile
                    for j in range(HK):
                        half, rec, split = s.half + j, s.rec + j, s.split + j
                        c = cell_c[:, s.layer, j, :]
                        dve.wait_ge(gate_act, tile + 2)
                        if s.first:
                            nc.vector.tensor_tensor(c, gates[:, s.layer, j, GATE_I, :], gates[:, s.layer, j, GATE_G, :], ALU.mult
                                                    ).then_inc(c_done, 1)
                        else:
                            nc.vector.tensor_tensor(ig[:, j, :], gates[:, s.layer, j, GATE_I, :], gates[:, s.layer, j, GATE_G, :],
                                                    ALU.mult).then_inc(ig_done, 1)
                            dve.wait_ge(gate_act, tile + 3)
                            nc.vector.tensor_tensor(c, gates[:, s.layer, j, GATE_F, :], c, ALU.mult).then_inc(fc_done, 1)
                            dve.wait_ge(ig_done, rec + 1)
                            dve.wait_ge(fc_done, rec + 1)
                            nc.vector.tensor_tensor(c, c, ig[:, j, :], ALU.add).then_inc(c_done, 1)
                        tile = tile + len(s.gates)
                        dve.wait_ge(gate_act, tile)
                        dve.wait_ge(tanh_c_done, half + 1)
                        o = gates[:, s.layer, j, GATE_O, :]
                        if s.last:
                            nc.vector.tensor_tensor(h_last[:, j, :], o, tanh_c[:, s.layer, j, :], ALU.mult
                                                    ).then_inc(h_done[s.layer], 1)
                            continue
                        hi = h_part[:, s.layer, s.write_slot, HI, j, :]
                        lo = h_part[:, s.layer, s.write_slot, LO, j, :]
                        nc.vector.tensor_tensor(h_full[:, j, :], o, tanh_c[:, s.layer, j, :], ALU.mult).then_inc(h_full_done, 1)
                        nc.vector.tensor_tensor(hi, o, tanh_c[:, s.layer, j, :], ALU.mult).then_inc(h_hi_done, 1)
                        dve.wait_ge(h_full_done, split + 1)
                        dve.wait_ge(h_hi_done, split + 1)
                        nc.vector.tensor_tensor(lo, h_full[:, j, :], hi, ALU.subtract).then_inc(h_done[s.layer], 1)
                elif kind == "head":
                    for g in range(GR):
                        dve.wait_ge(y_acc, s * GR + g + 1)
                        nc.vector.tensor_tensor(y[:, g, :], aux[:, g, :], b_head[:, :], ALU.add
                                                ).then_inc(y_put, 1)
                    if not isinstance(s, int):
                        dve.wait_ge(y_out, (s + 1) * GR * DMA)

        @block.tensor
        def _(pe):
            pe.wait_ge(proj_in, (5 + TT) * DMA)
            for s in range(TT):
                for k in range(TAPS):
                    at = PAD - (s + k) * D_FEAT
                    mm = nc.tensor.matmul(aux[0:KF, 0, s * D_CONV:(s + 1) * D_CONV], proj_t[:, at:at + KF],
                                          conv_w[:, k, :], start=(k == 0), stop=(k == TAPS - 1))
            mm.then_inc(band_acc, 1)
            for s in range(TT):
                for k in range(TAPS):
                    mm = nc.tensor.matmul(aux[s * D_CONV:(s + 1) * D_CONV, 1, 0:1], conv_w[:, k, :],
                                          proj_bias[:, :], start=(k == 0), stop=(k == TAPS - 1))
            mm.then_inc(band_acc, 1)

            pe.wait_ge(ident_ready, 1)
            pe.wait_ge(prep, 10)
            for m in range(M):
                mm = nc.tensor.transpose(acc[:, m // 4, (m % 4) * P:(m % 4 + 1) * P], wx_nat[:, m, :], ident[:, :])
                if m % 4 == 3:
                    mm.then_inc(wx_turned, 1)
            pe.wait_ge(ident16_ready, 1)
            for i in range(3):
                for part, ready in ((HI, part_hi), (LO, part_lo)):
                    pe.wait_ge(ready, i + 1)
                    for k in range(HK):
                        b = 2 * HK * i + HK * part + k
                        if b < 4:
                            pe.wait_ge(band_put, 2)
                        else:
                            pe.wait_ge(part_put, b - 3)
                        for m in range(M):
                            mm = nc.tensor.transpose(aux[:, b % 4, :].bitcast(F16)[:, m * P:(m + 1) * P],
                                                     w_part[:, part, m, k * P:(k + 1) * P], ident16[:, :])
                        mm.then_inc(part_turned, 1)

            pe.wait_ge(w1_in, 2 * DMA)
            for k in range(D1 // P):
                if k % 2 == 0:
                    pe.wait_ge(wx_lo_put, k // 2 + 1)
                for a in range(HK):
                    mm = nc.tensor.transpose(acc[:, k // 2, (k % 2 * HK + a) * P:(k % 2 * HK + a + 1) * P],
                                             w1_nat[:, a, k * P:(k + 1) * P], ident[:, :])
                if k % 2 == 1:
                    mm.then_inc(w1_turned, 1)
            pe.wait_ge(w1_put, 2)
            pe.wait_ge(w2_in, 2 * DMA)
            for m in range(D2 // P):
                if m >= 2:
                    pe.wait_ge(w12_put, 2 * (m - 1))
                for k in range(D1 // P):
                    mm = nc.tensor.matmul(acc[:, 2 + m % 2, 0:H + 1], w2[:, k, m * P:(m + 1) * P], w1_t[:, k, :],
                                          start=(k == 0), stop=(k == D1 // P - 1))
                mm.then_inc(w12_acc, 1)
            pe.wait_ge(w3_in, 2 * DMA)
            pe.wait_ge(w12_put, 2 * D2 // P)
            for a in range(HK):
                for k in range(D2 // P):
                    mm = nc.tensor.matmul(acc[:, a, :], w12_t[:, k, a * P:(a + 1) * P], w3[:, k, :],
                                          start=(k == 0), stop=(k == D2 // P - 1))
                mm.then_inc(head_acc, 1)
            pe.wait_ge(part_put, 12)
            for k in range(D2 // P):
                mm = nc.tensor.matmul(aux[:, 0, :], w12_t[:, k, H:H + 1].to_broadcast([P, P]), w3[:, k, :],
                                      start=(k == 0), stop=(k == D2 // P - 1))
            mm.then_inc(head_acc, 1)
            pe.wait_ge(head_put, HK + 1)

            for kind, s in stages(pe, NB, STEPS):
                if kind == "transpose":
                    pe.wait_ge(gathered, PER_GATHER * (s + 1))
                    pe.wait_ge(coords_put, s + 1)
                    for c in range(CH):
                        for g in range(GR):
                            mm = nc.tensor.transpose(
                                aux[0:KF, c, g * P:(g + 1) * P],
                                feat[:, g, c * TT:c * TT + WIN, :].rearrange("p t f -> p (t f)"), ident[:, :])
                    mm.then_inc(feat_turned, 1)
                    for g in range(GR):
                        mm = nc.tensor.transpose(aux[0:ROW_LOW, 2, g * P:(g + 1) * P], emb[:, g, :], ident[:, :])
                    mm.then_inc(emb_turned, 1)
                elif kind == "conv":
                    pe.wait_ge(feat_put, s + 1)
                    pe.wait_ge(emb_act, s + 1)
                    for c in range(CH):
                        mm = nc.tensor.matmul(aux[:, 2 + c, :], conv_band[:, :], feat_t[:, c, :], start=True, stop=True)
                    mm.then_inc(conv_acc, 1)
                elif kind == "cell":
                    upper = s.layer == 1
                    own_w = 2 if upper else 0
                    if not upper and s.first:
                        pe.wait_ge(x_put, (s.batch + 1) * PER_X)
                    for j in range(HK):
                        for g in s.gates:
                            m = g * HK + j
                            rows = slice(m * P, (m + 1) * P)
                            bank = acc[:, s.bank(j, g), :]
                            place = s.place(j, g)
                            opens = place == 0
                            if not (isinstance(s.tile, int) and s.tile + place < 4):
                                pe.wait_ge(gate_act, s.tile + place - 3)
                            if not upper:
                                for part in (HI, LO):
                                    mm = nc.tensor.matmul(bank, wx[:, part, rows], x_in[:, s.x_slot, s.t, :],
                                                          start=(part == HI), stop=(s.first and part == LO))
                            else:
                                for c in range(HK):
                                    if opens:
                                        pe.wait_ge(h_done[0], ahead + s.own + c + 1)
                                    for a, b in ((HI, HI), (HI, LO), (LO, HI)):
                                        mm = nc.tensor.matmul(bank, wh[:, 1, a, c, rows],
                                                              h_part[:, 0, s.write_slot, b, c, :],
                                                              start=(c == 0 and a == b == HI),
                                                              stop=(s.first and c == HK - 1 and a == LO))
                            if not s.first:
                                for c in range(HK):
                                    if opens:
                                        pe.wait_ge(h_done[s.layer], ahead + s.own + c - 1)
                                    for a, b in ((HI, HI), (HI, LO), (LO, HI)):
                                        mm = nc.tensor.matmul(bank, wh[:, own_w, a, c, rows],
                                                              h_part[:, s.layer, s.read_slot, b, c, :],
                                                              start=False, stop=(c == HK - 1 and a == LO))
                            mm.then_inc(gate_acc, 1)
                elif kind == "head":
                    pe.wait_ge(h_done[1], ahead + (s + 1) * 2 * STEPS)
                    for g in range(GR):
                        for c in range(HK):
                            mm = nc.tensor.matmul(aux[:, g, :], h_last[:, c, g * P:(g + 1) * P], w_head[:, c, :],
                                                  start=(c == 0), stop=(c == HK - 1))
                        mm.then_inc(y_acc, 1)


_PREFIX = "L0_rec_"
_OUT = (2048, 512)


def kernel(**inputs):
    import numpy as _np
    import concourse.bacc as _bacc
    from concourse import mybir as _mybir
    from concourse.bass_utils import run_bass_kernel_spmd as _run

    nc = _bacc.Bacc("TRN2", target_bir_lowering=False, num_devices=1)
    arrays, tensors = {}, {}
    for name, value in inputs.items():
        a = _np.ascontiguousarray(value)
        arrays[f"in_{name}"] = a
        tensors[name.replace(_PREFIX, "")] = nc.dram_tensor(f"in_{name}", a.shape, _mybir.dt.from_np(a.dtype),
                                                            kind="ExternalInput").ap()
    tensors["out"] = nc.dram_tensor("out_0", _OUT, _mybir.dt.from_np(_np.dtype("float32")),
                                    kind="ExternalOutput").ap()
    build(nc, tensors)
    return _run(nc, [arrays], core_ids=[0]).results[0]["out_0"]
```

```python
from contextlib import ExitStack

import concourse.bass as bass
from concourse import mybir

F32 = mybir.dt.float32
F32R = mybir.dt.float32r
F16 = mybir.dt.float16
BF16 = mybir.dt.bfloat16
I32 = mybir.dt.int32
ALU = mybir.AluOpType
ACT = mybir.ActivationFunctionType
AX = mybir.AxisListType

P = 128
NCOL = 512
GATE_I, GATE_F, GATE_G, GATE_O = range(4)
GATE_ORDER = (GATE_I, GATE_G, GATE_F, GATE_O)
HI, LO = 0, 1
DMA = 16

EXP_ONE = 1 << 23
EXP_MASK = 0x7F800000
EXP_LEAST = 121 * EXP_ONE
SCALE_FROM = (127 + 14 + 127) * EXP_ONE
UNSCALE_BY = 14 * EXP_ONE


class Cell:

    def __init__(self, layer, t, counts, bank0, before, slots=None, first=False, last=False, batch=None,
                 x_part=None):
        self.layer, self.t, self.first, self.last = layer, t, first, last
        self.batch, self.x_part = batch, x_part
        self.opens_f = layer == 0 and isinstance(t, int) and t == 1
        self.tile, self.half, self.rec, self.split = counts
        self.bank0 = bank0
        self.before = before
        self.read_slot, self.write_slot = slots if slots else ((t + 1) % 2, t % 2)
        self.gates = [g for g in GATE_ORDER if not (first and g == GATE_F)]

    def place(self, j, g):
        return j * len(self.gates) + self.gates.index(g)

    def bank(self, j, g):
        return (self.bank0 + self.place(j, g)) % 4


def stages(eng, nbatch, steps):
    snap = eng.snap
    last_t = steps - 1
    tiles, halves = 8 * steps - 2, 2 * steps

    class Base:

        def __init__(self, n):
            self.batch = n
            reg = (lambda v: v) if isinstance(n, int) else snap
            self.tiles, self.halves, self.recs = reg(n * tiles), reg(n * halves), reg(n * (halves - 2))

        def tile(self, t):
            return self.tiles + (8 * t - 2 if t else 0)

        def counts(self, layer, t):
            rec = self.recs + (2 * t - 2 if t else 0)
            return self.tile(t), self.halves + 2 * t, rec, (self.halves if layer == 0 else self.recs) + 2 * t

    def cell(base, layer, t, bank0, before):
        x_part = {(0, 0): 0, (0, 1): 1, (1, 0): 2}.get((layer, t))
        return "cell", Cell(layer, t, base.counts(layer, t), bank0, before, first=(t == 0),
                            last=(layer == 1 and t == last_t), batch=base.batch, x_part=x_part)

    def body(n, following):
        base = Base(n)
        bank = 14 % 4
        yield cell(base, 1, 0, bank, (0, base.tile(2)))
        bank = (bank + 6) % 4
        with eng.Fori(0, steps - 3) as u:
            t = snap(u + 2)
            even, odd = snap(t % 2), snap((u + 1) % 2)
            tile, half = snap(base.tiles + u * 8 + 6), snap(base.halves + u * 2 + 2)
            rec = snap(base.recs + u * 2)
            yield "cell", Cell(0, t, (tile + 8, half + 2, rec + 2, half + 2), bank, (1, tile), slots=(odd, even))
            yield "cell", Cell(1, None, (tile, half, rec, rec + 2), bank, (0, tile + 16), slots=(even, odd))
        if following:
            yield "turn", n + 1, 0
            yield "turn", n + 1, 1
            yield "turn_emb", n + 1
        yield cell(base, 0, last_t, bank, (1, base.tile(last_t - 1)))
        if following:
            yield "conv", n + 1, 0
            yield "emb_gates", n + 1, 0
        yield cell(base, 1, last_t - 1, bank, (0, base.tiles + tiles))
        before = (0, base.tiles + tiles)
        if following:
            yield "emb_gates", n + 1, 1
            after = Base(n + 1)
            yield cell(after, 0, 0, bank, (1, base.tile(last_t)))
            bank = (bank + 6) % 4
            before = (0, after.tile(1))
            yield "conv", n + 1, 1
            yield "emb_gates", n + 1, 2
            yield cell(base, 1, last_t, bank, before)
            yield cell(after, 0, 1, bank, (1, base.tiles + tiles))
        else:
            yield cell(base, 1, last_t, bank, (1, base.tile(last_t)))
        yield "head", n

    assert tiles * 2 % 4 == 0
    base = Base(0)
    yield "turn", 0, 0
    yield "turn_emb", 0
    yield "conv", 0, 0
    yield "head_weights", 0
    yield "emb_gates", 0, 0
    yield "head_weights", 1
    yield "emb_gates", 0, 1
    yield cell(base, 0, 0, 0, None)
    yield "turn", 0, 1
    yield "conv", 0, 1
    yield "emb_gates", 0, 2
    yield cell(base, 0, 1, 6 % 4, (0, base.tile(1)))
    with eng.Fori(0, nbatch - 1) as n:
        yield from body(n, True)
    yield from body(nbatch - 1, False)


def build(nc, d):
    B, T, _ = d["r_coords"].shape
    REG, D_REG = d["region_tbl"].shape
    POI, D_POI = d["poi_tbl"].shape
    CAR, D_CAR = d["car_tbl"].shape
    WEEK, D_WEEK = d["week_tbl"].shape
    TIME, D_TIME = d["time_tbl"].shape
    D_RP = d["W_rp"].shape[1]
    D_CO = d["W_co"].shape[1]
    TAPS, D_NV, D_CONV = d["conv_w"].shape
    D_FEAT = D_REG + D_POI + 2
    D_EMB = D_CAR + D_WEEK + D_TIME
    D_X = D_CONV + D_EMB
    GATES, H = d["Whh0"].shape
    HK = H // P
    M = GATES // P
    D1, D2, D3 = d["W1"].shape[1], d["W2"].shape[1], d["W3"].shape[1]
    STEPS = T - TAPS + 1
    NB = B // NCOL
    GR = NCOL // P
    TT = P // D_CONV
    CH = STEPS // TT
    WIN = (TT + TAPS - 1)
    KF = WIN * D_FEAT
    Q = 32
    assert HK == 2 and M == 8 and CH == 2 and D_RP + D_CO == D_NV and D_CONV == Q and D_EMB <= Q
    assert POI & (POI - 1) == 0

    with ExitStack() as ctx:
        def sb(name, shape, dt, stack=ctx):
            return stack.enter_context(nc.sbuf_tensor(name, shape, dt))

        def sem(name):
            return ctx.enter_context(nc.semaphore(name))

        idx_raw = {"region": sb("region_raw", [P, NB * GR, T], I32), "poi": sb("poi_raw", [P, NB * GR, T], I32),
                   "car": sb("car_raw", [P, NB * GR, 1], I32), "week": sb("week_raw", [P, NB * GR, 1], I32),
                   "time": sb("time_raw", [P, NB * GR, 1], I32)}
        idx_wrap = sb("idx_wrap", [P, NB * GR, T], F32)
        idx = {k: sb(f"{k}_idx", list(v.shape), I32) for k, v in idx_raw.items()}
        coords = sb("coords", [P, NB * GR, T * 2], F32)
        feat = sb("feat", [P, GR, T, D_FEAT], F32)
        emb = sb("emb", [P, GR, 4, Q], F32)
        feat_t = sb("feat_t", [KF, CH, NCOL], F32)
        relu_part = sb("relu_part", [P, NCOL], F32)
        neg_part = sb("neg_part", [P, NCOL], F32)
        tanh_part = sb("tanh_part", [P, NCOL], F32)
        conv_hi = sb("conv_hi", [P, CH, NCOL], F32R)
        conv_lo = sb("conv_lo", [P, CH, NCOL], F32R)
        emb_tanh = sb("emb_tanh", [P, NCOL], F32)
        emb_in = sb("emb_in", [P, NCOL], F32R)
        wx = sb("wx", [3 * Q, GATES], F32R)
        we = sb("we", [P, GATES], F32R)
        wh = sb("wh", [P, 3, 2, HK, GATES], F16)
        w_head = sb("w_head", [P, HK, D3], F32)
        b_head = sb("b_head", [P, D3], F32)
        conv_band = sb("conv_band", [KF, P], F32)
        conv_bias = sb("conv_bias", [P, 1], F32)
        gate_bias = sb("gate_bias", [P, 2, M], F32)
        unscale = sb("unscale", [P, 2, M], F32)
        ident = sb("ident", [P, P], F32)
        ident16 = sb("ident16", [P, P], F16)
        before_first = sb("before_first", [P, 1], F32)

        with ExitStack() as early:
            poi_all = sb("poi_all", [POI, NCOL * T], I32, early)
            poi_hot = sb("poi_hot", [POI, NCOL * T], BF16, early)
        x_in = sb("x_in", [3 * Q, STEPS, NCOL], F32R)
        emb_gates = sb("emb_gates", [P, M, NCOL], F32)

        with ExitStack() as setup:
            w_nat = sb("w_nat", [P, 3, M, H], F32, setup)
            wx_nat = sb("wx_nat", [P, M, 7 * Q], F32, setup)
            w_part = sb("w_part", [P, 2, M, H], F16, setup)
            w1_nat = sb("w1_nat", [P, HK, D1], F32, setup)
            w1_t = sb("w1_t", [P, D1 // P, H + 1], F32, setup)
            w2 = sb("w2", [P, D1 // P, D2], F32, setup)
            w3 = sb("w3", [P, D2 // P, D3], F32, setup)
            w12_t = sb("w12_t", [P, D2 // P, H + 1], F32, setup)
            b2_col = sb("b2_col", [P, D2 // P], F32, setup)
            b3_row = sb("b3_row", [P, D3], F32, setup)
            bias_in = sb("bias_in", [P, 2, 2, M], F32, setup)
            row_max = sb("row_max", [P, 3, M], F32, setup)
            exp_bits = sb("exp_bits", [P, 2, M], I32, setup)
            row_scale = sb("row_scale", [P, 2, M], F32, setup)
            PAD = (WIN - 1) * D_FEAT
            proj_t = sb("proj_t", [D_NV, PAD + D_FEAT + PAD], F32, setup)
            conv_w = sb("conv_w", [D_NV, TAPS, D_CONV], F32, setup)
            proj_bias = sb("proj_bias", [D_NV, 1], F32, setup)
            conv_b = sb("conv_b", [P, 1], F32, setup)
            poi_tbl = sb("poi_tbl", [POI, D_POI], F32, setup)
            poi_rest = sb("poi_rest", [POI, 2, D_POI], F32, setup)
            poi_part = sb("poi_part", [POI, 3, D_POI], BF16, setup)
            poi_sum = sb("poi_sum", [P, GR * T, D_POI], F32, setup)
            poi_number = sb("poi_number", [POI, 1], F32, setup)

        gates = sb("gates", [P, 2, HK, 4, NCOL], F32)
        ig = sb("ig", [P, HK, NCOL], F32)
        cell_c = sb("cell_c", [P, 2, HK, NCOL], F32)
        tanh_c = sb("tanh_c", [P, 2, HK, NCOL], F32)
        h_full = sb("h_full", [P, HK, NCOL], F32)
        h_part = sb("h_part", [P, 2, 2, 2, HK, NCOL], F16)
        h_last = sb("h_last", [P, HK, NCOL], F32)
        y = sb("y", [P, GR, D3], F32)

        acc = ctx.enter_context(nc.psum_tensor("acc", [P, 4, NCOL], F32))
        aux = ctx.enter_context(nc.psum_tensor("aux", [P, 4, NCOL], F32))

        idx_in = {k: sem(f"{k}_in") for k in idx_raw}
        coords_in = sem("coords_in")
        poi_all_in, poi_tbl_in = sem("poi_all_in"), sem("poi_tbl_in")
        w_in = [sem(f"w_in{i}") for i in range(3)]
        wx_in = sem("wx_in")
        bias_loaded = sem("bias_loaded")
        proj_in = sem("proj_in")
        w1_in, w2_in, w3_in = sem("w1_in"), sem("w2_in"), sem("w3_in")
        rows_in = [sem("rows0_in"), sem("rows1_in")]
        emb_rows_in = sem("emb_rows_in")
        zeroed = sem("zeroed")
        ident_zero, ident_ready, ident16_ready = sem("ident_zero"), sem("ident_ready"), sem("ident16_ready")
        idx_step, idx_ready = sem("idx_step"), sem("idx_ready")
        number_ready = sem("number_ready")
        poi_step, poi_hot_ready, poi_acc, poi_put = sem("poi_step"), sem("poi_hot_ready"), sem("poi_acc"), sem("poi_put")
        coords_put = sem("coords_put")
        emb_copied = sem("emb_copied")
        prep = sem("prep")
        wx_scaled, scaled = sem("wx_scaled"), sem("scaled")
        part_hi, part_lo = sem("part_hi"), sem("part_lo")
        part_turned = sem("part_turned")
        part_put = sem("part_put")
        band_acc, band_put = sem("band_acc"), sem("band_put")
        wx_turned, wx_hi_put, wx_lo_put = sem("wx_turned"), sem("wx_hi_put"), sem("wx_lo_put")
        w1_turned, w1_put = sem("w1_turned"), sem("w1_put")
        w12_acc, w12_put = sem("w12_acc"), sem("w12_put")
        head_acc, head_put = sem("head_acc"), sem("head_put")
        turned, turned_put = [sem("turned0"), sem("turned1")], [sem("turned0_put"), sem("turned1_put")]
        emb_turned, emb_act, emb_step, emb_ready = sem("emb_turned"), sem("emb_act"), sem("emb_step"), sem("emb_ready")
        emb_gates_acc, emb_gates_put = sem("emb_gates_acc"), sem("emb_gates_put")
        conv_acc = sem("conv_acc")
        relu_done, neg_done, tanh_done = sem("relu_done"), sem("neg_done"), sem("tanh_done")
        elu_step, conv_hi_put, conv_lo_put = sem("elu_step"), sem("conv_hi_put"), sem("conv_lo_put")
        x_put = [sem("x0_put"), sem("x1_put"), sem("x2_put")]
        def both(name):
            return [sem(f"{name}{layer}") for layer in range(2)]

        gate_acc, gate_act = both("gate_acc"), both("gate_act")
        gate_sum = sem("gate_sum")
        ig_done, fc_done, c_done, tanh_c_done = both("ig_done"), both("fc_done"), both("c_done"), both("tanh_c_done")
        h_full_done, h_hi_done, h_done = both("h_full_done"), both("h_hi_done"), both("h_done")
        y_acc, y_put, y_out = sem("y_acc"), sem("y_put"), sem("y_out")

        ahead = 2
        TABLES_FIRST, TABLES = 1, 2
        OWN_STEPS = (WIN, T - WIN)
        tables = {"region": d["region_tbl"], "poi": d["poi_tbl"], "car": d["car_tbl"],
                  "week": d["week_tbl"], "time": d["time_tbl"]}
        EMB_PARTS = [[(j, g, i) for i, g in enumerate((GATE_I, GATE_G, GATE_O))] for j in range(HK)]
        EMB_PARTS.append([(j, GATE_F, 2 * j) for j in range(HK)])
        EMB_BEFORE = (0, 3, 6)
        acc_read = (gate_sum, gate_act[1])
        X_DMAS = (3 * DMA, 3 * (TT - 1) * DMA, 3 * TT * DMA)

        def is_first(n):
            return isinstance(n, int) and n == 0

        def rows_count(n, c):
            return (n * TABLES + TABLES_FIRST) * GR * OWN_STEPS[c] * DMA

        block = ctx.enter_context(nc.Block())

        @block.sync
        def _(sp):
            def load(out, src, loaded):
                sp.dma_start(out, src, allow_slow_non_contiguous=True).then_inc(loaded, DMA)

            def load_rows(k):
                load(idx_raw[k][:, :, :].rearrange("p (n g) t -> p n g t", g=GR),
                     d[f"r_{k}_idx"].rearrange("(n p g) t -> p n g t", p=P, g=GR), idx_in[k])

            load_rows("region")
            for k in ("car", "week", "time"):
                load(idx_raw[k][:, :, 0].rearrange("p (n g) -> p n g", g=GR),
                     d[f"r_{k}_idx"].rearrange("(n p g) -> p n g", p=P, g=GR), idx_in[k])
            load(poi_all[:, :], d["r_poi_idx"][0:NCOL, :].rearrange("(a b) t -> a (b t)", a=1)
                 .partition_broadcast(POI)[:, 0, :], poi_all_in)
            load(poi_tbl[:, :], d["poi_tbl"], poi_tbl_in)
            sp.wait_ge(zeroed, 3)
            load(proj_t[0:D_RP, PAD:PAD + D_REG + D_POI], d["W_rp"].rearrange("i o -> o i"), proj_in)
            load(proj_t[D_RP:D_NV, PAD + D_REG + D_POI:PAD + D_FEAT], d["W_co"].rearrange("i o -> o i"), proj_in)
            load(conv_w[:, :, :], d["conv_w"].rearrange("k i o -> i k o"), proj_in)
            load(proj_bias[0:D_RP, 0], d["b_rp"], proj_in)
            load(proj_bias[D_RP:D_NV, 0], d["b_co"], proj_in)
            for k in range(TT):
                load(conv_b[k * D_CONV:(k + 1) * D_CONV, 0], d["conv_b"], proj_in)
            load(coords[:, :, :].rearrange("p (n g) x -> p n g x", g=GR),
                 d["r_coords"].rearrange("(n p g) t c -> p n g (t c)", p=P, g=GR), coords_in)
            load_rows("poi")
            load(w_nat[:, 0, :, :], d["Whh0"].rearrange("(m p) k -> p m k", p=P), w_in[0])
            wih0 = d["Wih0"].rearrange("(m p) k -> p m k", p=P)
            for q in range(3):
                load(wx_nat[:, :, q * Q:q * Q + D_CONV], wih0[:, :, 0:D_CONV], wx_in)
            for q in range(3, 7):
                load(wx_nat[:, :, q * Q:q * Q + D_EMB], wih0[:, :, D_CONV:D_X], wx_in)
            load(w1_nat[:, :, :], d["W1"].rearrange("(a p) n -> p a n", p=P), w1_in)
            load(w1_t[:, :, H], d["b1"].rearrange("(k p) -> p k", p=P), w1_in)
            load(w2[:, :, :], d["W2"].rearrange("(k p) n -> p k n", p=P), w2_in)
            load(b2_col[:, :], d["b2"].rearrange("(k p) -> p k", p=P), w2_in)
            for i, k in ((1, "Wih1"), (2, "Whh1")):
                load(w_nat[:, i, :, :], d[k].rearrange("(m p) k -> p m k", p=P), w_in[i])
            for layer in range(2):
                for i, k in enumerate(("bih", "bhh")):
                    load(bias_in[:, layer, i, :], d[f"{k}{layer}"].rearrange("(m p) -> p m", p=P), bias_loaded)
            load(w3[:, :, :], d["W3"].rearrange("(k p) n -> p k n", p=P), w3_in)
            load(b3_row[:, :], d["b3"].rearrange("(a n) -> a n", a=1).partition_broadcast(P)[:, 0, :], w3_in)

            out_rows = d["out"].rearrange("(n p g) o -> p n g o", p=P, g=GR)
            for stage in stages(sp, NB, STEPS):
                kind = stage[0]
                if kind == "conv":
                    n, c = stage[1:]
                    sp.wait_ge(conv_hi_put, n * CH + c + 1)
                    sp.wait_ge(conv_lo_put, n * CH + c + 1)
                    for k in range(TT):
                        t = c * TT + k
                        put = x_put[0 if t == 0 else c + 1]
                        for q, part in enumerate((conv_hi, conv_lo, conv_hi)):
                            sp.dma_start(x_in[q * Q:(q + 1) * Q, t, :].bitcast(F32),
                                         part[k * D_CONV:(k + 1) * D_CONV, c, :].bitcast(F32)).then_inc(put, DMA)
                elif kind == "head":
                    n = stage[1]
                    for g in range(GR):
                        sp.wait_ge(y_put, n * GR + g + 1)
                        sp.dma_start(out_rows[:, n, g, :], y[:, g, :]).then_inc(y_out, DMA)
            sp.wait_ge(y_out, NB * GR * DMA)

        @block.gpsimd
        def _(pool):
            nc.gpsimd.memset(emb[:, :, 0, D_EMB:Q], 0.0).then_inc(zeroed, 1)
            nc.gpsimd.memset(wx_nat[:, :, 3 * Q:7 * Q].rearrange("p m (q k) -> p m q k", k=Q)[:, :, :, D_EMB:Q], 0.0
                             ).then_inc(zeroed, 1)
            nc.gpsimd.memset(proj_t[:, :], 0.0).then_inc(zeroed, 1)
            nc.gpsimd.memset(ident[:, :], 0.0).then_inc(ident_zero, 1)
            pool.wait_ge(ident_zero, 1)
            nc.gpsimd.affine_select(out=ident[:, :], in_=ident[:, :], compare_op=ALU.not_equal, fill=1.0,
                                    base=0, pattern=[[-1, P]], channel_multiplier=1).then_inc(ident_ready, 1)
            nc.gpsimd.iota(poi_number[:, :], pattern=[[0, 1]], base=0, channel_multiplier=1,
                           allow_small_or_imprecise_dtypes=True).then_inc(number_ready, 1)
            pool.wait_ge(zeroed, 3)

            for n in range(NB):
                if n:
                    for c in range(CH):
                        pool.wait_ge(turned[c], n)
                    pool.wait_ge(emb_turned, n)

                def gather(k, out, g, t, landed):
                    pool.indirect_dma_start(out, None, tables[k],
                                            bass.IndirectOffsetOnAxis(ap=idx[k][:, n * GR + g, t:t + 1], axis=0)
                                            ).then_inc(landed, DMA)

                def gather_steps(c):
                    begin = 0 if c == 0 else OWN_STEPS[0]
                    for g in range(GR):
                        for t in range(begin, begin + OWN_STEPS[c]):
                            gather("region", feat[:, g, t, 0:D_REG], g, t, rows_in[c])
                            if n:
                                gather("poi", feat[:, g, t, D_REG:D_REG + D_POI], g, t, rows_in[c])

                if n == 0:
                    pool.wait_ge(idx_ready, 1)
                gather_steps(0)
                if n == 0:
                    pool.wait_ge(coords_in, DMA)
                nc.gpsimd.tensor_copy(feat[:, :, :, D_REG + D_POI:D_FEAT],
                                      coords[:, n * GR:(n + 1) * GR, :].rearrange("p g (t c) -> p g t c", c=2)
                                      ).then_inc(coords_put, 1)
                if n == 0:
                    pool.wait_ge(idx_ready, 4)
                for g in range(GR):
                    gather("car", emb[:, g, 0, 0:D_CAR], g, 0, emb_rows_in)
                    gather("week", emb[:, g, 0, D_CAR:D_CAR + D_WEEK], g, 0, emb_rows_in)
                    gather("time", emb[:, g, 0, D_CAR + D_WEEK:D_EMB], g, 0, emb_rows_in)
                pool.wait_ge(emb_rows_in, (n + 1) * 3 * GR * DMA)
                nc.gpsimd.tensor_copy(emb[:, :, 1:4, :], emb[:, :, 0, :].unsqueeze(2).to_broadcast([P, GR, 3, Q])
                                      ).then_inc(emb_copied, 1)
                if n == 0:
                    pool.wait_ge(idx_ready, 5)
                gather_steps(1)

        @block.scalar
        def _(act):
            for b in range(2):
                act.wait_ge(w1_turned, b + 1)
                nc.scalar.copy(w1_t[:, 2 * b:2 * b + 2, 0:H],
                               acc[:, b, :].rearrange("p (k a) -> p k a", k=2)).then_inc(w1_put, 1)
            act.wait_ge(w2_in, 2 * DMA)
            for m in range(D2 // P):
                act.wait_ge(w12_acc, m + 1)
                nc.scalar.copy(w12_t[:, m, 0:H], acc[:, m % 4, 0:H]).then_inc(w12_put, 1)
                nc.scalar.activation(w12_t[:, m, H:H + 1], acc[:, m % 4, H:H + 1], ACT.Identity,
                                     bias=b2_col[:, m:m + 1]).then_inc(w12_put, 1)
            for i in range(3):
                act.wait_ge(scaled, i + 1)
                if i:
                    act.wait_ge(part_turned, 2 * HK * i)
                nc.scalar.copy(w_part[:, HI, :, :], w_nat[:, i, :, :]).then_inc(part_hi, 1)
                for part in (HI, LO):
                    for k in range(HK):
                        b = 2 * HK * i + HK * part + k
                        act.wait_ge(part_turned, b + 1)
                        nc.scalar.copy(wh[:, i, part, k, :], aux[:, b % 4, :].bitcast(F16)).then_inc(part_put, 1)
            act.wait_ge(prep, 9)
            act.wait_ge(band_put, 2)

            for stage in stages(act, NB, STEPS):
                kind = stage[0]
                if kind == "turn_emb":
                    n = stage[1]
                    act.wait_ge(emb_turned, n + 1)
                    if not is_first(n):
                        act.wait_ge(emb_ready, n * 2)
                    nc.scalar.activation(emb_tanh[:, :], aux[:, 2, :], ACT.Tanh).then_inc(emb_act, 1)
                elif kind == "emb_gates":
                    n, part = stage[1:]
                    for i, (j, g, bank) in enumerate(EMB_PARTS[part]):
                        act.wait_ge(emb_gates_acc, n * M + EMB_BEFORE[part] + i + 1)
                        nc.scalar.copy(emb_gates[:, g * HK + j, :], aux[:, bank, :]).then_inc(emb_gates_put, 1)
                elif kind == "conv":
                    n, c = stage[1:]
                    chunk = n * CH + c
                    act.wait_ge(conv_acc, chunk + 1)
                    if not (is_first(n) and c == 0):
                        act.wait_ge(conv_lo_put, chunk)
                    nc.scalar.activation(relu_part[:, :], aux[:, 3, :], ACT.Relu,
                                         bias=conv_bias[:, 0:1]).then_inc(relu_done, 1)
                    act.wait_ge(neg_done, chunk + 1)
                    nc.scalar.activation(tanh_part[:, :], neg_part[:, :], ACT.Tanh, scale=0.5
                                         ).then_inc(tanh_done, 1)
                elif kind == "head_weights" and stage[1] == 0:
                    for a in range(HK):
                        act.wait_ge(head_acc, a + 1)
                        nc.scalar.copy(w_head[:, a, :], acc[:, a, :]).then_inc(head_put, 1)
                elif kind == "cell":
                    s = stage[1]
                    layer = s.layer
                    for j in range(HK):
                        if layer == 1:
                            act.wait_ge(h_done[1], ahead + s.half + j - 1)
                        for g in s.gates:
                            count = s.tile + s.place(j, g) + 1
                            if layer == 0:
                                act.wait_ge(gate_sum, count)
                                source = gates[:, 0, j, g, :]
                            else:
                                act.wait_ge(gate_acc[1], count)
                                source = acc[:, s.bank(j, g), :]
                            m = g * HK + j
                            nc.scalar.activation(gates[:, layer, j, g, :], source,
                                                 ACT.Tanh if g == GATE_G else ACT.Sigmoid,
                                                 bias=gate_bias[:, layer, m:m + 1],
                                                 scale=unscale[:, layer, m:m + 1]).then_inc(gate_act[layer], 1)
                        act.wait_ge(c_done[layer], s.half + j + 1)
                        nc.scalar.activation(tanh_c[:, layer, j, :], cell_c[:, layer, j, :], ACT.Tanh
                                             ).then_inc(tanh_c_done[layer], 1)

        @block.vector
        def _(dve):
            nc.vector.memset(before_first[:, :], 0.0).then_inc(h_done[1], ahead)
            def indices(i, k, rows):
                dve.wait_ge(idx_in[k], DMA)
                raw = idx_raw[k]
                wrap = idx_wrap[:, :, 0:raw.shape[2]]
                if i:
                    dve.wait_ge(idx_ready, i)
                nc.vector.tensor_scalar(wrap, raw[:, :, :], 0.0, float(rows), ALU.is_lt, ALU.mult
                                        ).then_inc(idx_step, 1)
                dve.wait_ge(idx_step, 2 * i + 1)
                nc.vector.tensor_tensor(wrap, wrap, raw[:, :, :], ALU.add).then_inc(idx_step, 1)
                dve.wait_ge(idx_step, 2 * i + 2)
                nc.vector.tensor_scalar(idx[k][:, :, :], wrap, 0.0, float(rows - 1), ALU.max, ALU.min
                                        ).then_inc(idx_ready, 1)

            indices(0, "region", REG)
            indices(1, "car", CAR)
            indices(2, "week", WEEK)
            indices(3, "time", TIME)

            dve.wait_ge(poi_all_in, DMA)
            nc.vector.tensor_scalar(poi_all[:, :], poi_all[:, :], float(-POI), float(POI - 1), ALU.max, ALU.min
                                    ).then_inc(poi_step, 1)
            dve.wait_ge(poi_step, 1)
            nc.vector.tensor_scalar(poi_all[:, :], poi_all[:, :], POI - 1, None, ALU.bitwise_and
                                    ).then_inc(poi_step, 1)
            dve.wait_ge(poi_step, 2)
            dve.wait_ge(number_ready, 1)
            nc.vector.tensor_scalar(poi_hot[:, :], poi_all[:, :], poi_number[:, 0:1], None, ALU.is_equal
                                    ).then_inc(poi_hot_ready, 1)
            dve.wait_ge(poi_tbl_in, DMA)
            rest = poi_tbl
            for i in range(3):
                nc.vector.tensor_copy(poi_part[:, i, :], rest[:, :] if i == 0 else poi_rest[:, i - 1, :]
                                      ).then_inc(poi_hot_ready, 1)
                if i < 2:
                    dve.wait_ge(poi_hot_ready, i + 2)
                    nc.vector.tensor_tensor(poi_rest[:, i, :], rest[:, :] if i == 0 else poi_rest[:, i - 1, :],
                                            poi_part[:, i, :], ALU.subtract).then_inc(poi_step, 1)
                    dve.wait_ge(poi_step, i + 3)

            dve.wait_ge(band_acc, 2)
            nc.vector.tensor_copy(conv_band[:, :], aux[0:KF, 0, 0:P]).then_inc(band_put, 1)
            nc.vector.tensor_tensor(conv_bias[:, :], aux[:, 1, 0:1], conv_b[:, :], ALU.add).then_inc(band_put, 1)
            dve.wait_ge(ident_ready, 1)
            nc.vector.tensor_copy(ident16[:, :], ident[:, :]).then_inc(ident16_ready, 1)

            dve.wait_ge(poi_acc, 1)
            part_rows = aux[:, 3, 0:GR * T * 3 * D_POI].rearrange("p (r s) -> p r s", s=3 * D_POI)
            nc.vector.tensor_copy(poi_sum[:, :, :], part_rows[:, :, 2 * D_POI:3 * D_POI]).then_inc(poi_step, 1)
            dve.wait_ge(poi_step, 5)
            nc.vector.tensor_tensor(poi_sum[:, :, :], poi_sum[:, :, :], part_rows[:, :, D_POI:2 * D_POI], ALU.add
                                    ).then_inc(poi_step, 1)
            dve.wait_ge(poi_step, 6)
            nc.vector.tensor_tensor(feat[:, :, :, D_REG:D_REG + D_POI],
                                    poi_sum[:, :, :].rearrange("p (g t) f -> p g t f", g=GR),
                                    part_rows[:, :, 0:D_POI].rearrange("p (g t) f -> p g t f", g=GR), ALU.add
                                    ).then_inc(poi_put, 1)

            for i in range(3):
                dve.wait_ge(w_in[i], DMA)
                nc.vector.tensor_reduce(row_max[:, i, :], w_nat[:, i, :, :], AX.X, ALU.max,
                                        apply_absolute_value=True).then_inc(prep, 1)
            dve.wait_ge(prep, 3)
            nc.vector.tensor_tensor(row_max[:, 1, :], row_max[:, 1, :], row_max[:, 2, :], ALU.max).then_inc(prep, 1)
            dve.wait_ge(prep, 4)
            nc.vector.tensor_scalar(exp_bits[:, :, :], row_max[:, 0:2, :].bitcast(I32), EXP_MASK, None,
                                    ALU.bitwise_and).then_inc(prep, 1)
            dve.wait_ge(prep, 5)
            nc.vector.tensor_scalar(exp_bits[:, :, :], exp_bits[:, :, :], float(EXP_LEAST), None, ALU.max
                                    ).then_inc(prep, 1)
            dve.wait_ge(prep, 6)
            nc.vector.tensor_scalar(row_scale[:, :, :].bitcast(I32), exp_bits[:, :, :], -1.0, float(SCALE_FROM),
                                    ALU.mult, ALU.add).then_inc(prep, 1)
            nc.vector.tensor_scalar(unscale[:, :, :].bitcast(I32), exp_bits[:, :, :], float(-UNSCALE_BY), None,
                                    ALU.add).then_inc(prep, 1)
            dve.wait_ge(bias_loaded, 4 * DMA)
            nc.vector.tensor_tensor(gate_bias[:, :, :], bias_in[:, :, 0, :], bias_in[:, :, 1, :], ALU.add
                                    ).then_inc(prep, 1)
            dve.wait_ge(prep, 9)

            def scale_weights(i):
                layer = 0 if i == 0 else 1
                nc.vector.tensor_tensor(w_nat[:, i, :, :], w_nat[:, i, :, :],
                                        row_scale[:, layer, :].unsqueeze(2).to_broadcast([P, M, H]), ALU.mult
                                        ).then_inc(scaled, 1)

            def low_parts(i):
                dve.wait_ge(part_hi, i + 1)
                nc.vector.tensor_tensor(w_part[:, LO, :, :], w_nat[:, i, :, :], w_part[:, HI, :, :], ALU.subtract
                                        ).then_inc(part_lo, 1)

            scale_weights(0)
            dve.wait_ge(wx_in, 7 * DMA)
            nc.vector.tensor_tensor(wx_nat[:, :, :], wx_nat[:, :, :],
                                    row_scale[:, 0, :].unsqueeze(2).to_broadcast([P, M, 7 * Q]), ALU.mult
                                    ).then_inc(wx_scaled, 1)
            low_parts(0)
            scale_weights(1)
            for b in range(4):
                out, rows = (wx, 3 * Q) if b < 2 else (we, 4 * Q)
                cols = slice(b % 2 * NCOL, (b % 2 + 1) * NCOL)
                dve.wait_ge(wx_turned, b + 1)
                nc.vector.tensor_copy(out[0:rows, cols], acc[0:rows, b, :]).then_inc(wx_hi_put, 1)
                dve.wait_ge(wx_hi_put, b + 1)
                nc.vector.tensor_tensor(out[2 * Q:rows, cols], acc[2 * Q:rows, b, :],
                                        out[2 * Q:rows, cols].bitcast(F32), ALU.subtract).then_inc(wx_lo_put, 1)
            low_parts(1)
            scale_weights(2)
            low_parts(2)
            indices(4, "poi", POI)

            def add_embeddings(s, j, g):
                dve.wait_ge(gate_acc[0], s.tile + s.place(j, g) + 1)
                nc.vector.tensor_tensor(gates[:, 0, j, g, :], acc[:, s.bank(j, g), :], emb_gates[:, g * HK + j, :],
                                        ALU.add).then_inc(gate_sum, 1)

            for stage in stages(dve, NB, STEPS):
                kind = stage[0]
                if kind == "turn":
                    n, c = stage[1:]
                    dve.wait_ge(turned[c], n + 1)
                    nc.vector.tensor_copy(feat_t[:, c, :], aux[0:KF, c, :]).then_inc(turned_put[c], 1)
                elif kind == "turn_emb":
                    n = stage[1]
                    dve.wait_ge(emb_act, n + 1)
                    nc.vector.tensor_copy(emb_in[:, :], emb_tanh[:, :]).then_inc(emb_step, 1)
                    dve.wait_ge(emb_step, n + 1)
                    for q in (1, 3):
                        rows = slice(q * Q, (q + 1) * Q)
                        nc.vector.tensor_tensor(emb_in[rows, :], emb_tanh[rows, :], emb_in[rows, :].bitcast(F32),
                                                ALU.subtract).then_inc(emb_ready, 1)
                elif kind == "conv":
                    n, c = stage[1:]
                    chunk = n * CH + c
                    dve.wait_ge(relu_done, chunk + 1)
                    nc.vector.tensor_scalar(neg_part[:, :], aux[:, 3, :], conv_bias[:, 0:1], 0.0,
                                            ALU.add, ALU.min).then_inc(neg_done, 1)
                    dve.wait_ge(tanh_done, chunk + 1)
                    nc.vector.tensor_scalar(neg_part[:, :], tanh_part[:, :], -1.0, 1.0, ALU.mult, ALU.add
                                            ).then_inc(elu_step, 1)
                    dve.wait_ge(elu_step, chunk * 4 + 1)
                    nc.vector.reciprocal(neg_part[:, :], neg_part[:, :]).then_inc(elu_step, 1)
                    dve.wait_ge(elu_step, chunk * 4 + 2)
                    nc.vector.scalar_tensor_tensor(neg_part[:, :], tanh_part[:, :], 2.0, neg_part[:, :],
                                                   ALU.mult, ALU.mult).then_inc(elu_step, 1)
                    dve.wait_ge(elu_step, chunk * 4 + 3)
                    nc.vector.tensor_tensor(relu_part[:, :], relu_part[:, :], neg_part[:, :], ALU.add
                                            ).then_inc(elu_step, 1)
                    dve.wait_ge(elu_step, chunk * 4 + 4)
                    if not is_first(n):
                        for i in ((0, 1) if c == 0 else (2,)):
                            dve.wait_ge(x_put[i], n * X_DMAS[i])
                    nc.vector.tensor_copy(conv_hi[:, c, :], relu_part[:, :]).then_inc(conv_hi_put, 1)
                    dve.wait_ge(conv_hi_put, chunk + 1)
                    nc.vector.tensor_tensor(conv_lo[:, c, :], relu_part[:, :], conv_hi[:, c, :].bitcast(F32),
                                            ALU.subtract).then_inc(conv_lo_put, 1)
                elif kind == "head_weights" and stage[1] == 1:
                    dve.wait_ge(head_acc, HK + 1)
                    dve.wait_ge(w3_in, 2 * DMA)
                    nc.vector.tensor_tensor(b_head[:, :], acc[:, HK, :], b3_row[:, :], ALU.add).then_inc(head_put, 1)
                elif kind == "cell":
                    s = stage[1]
                    layer = s.layer
                    for j in range(HK):
                        half, rec, split = s.half + j, s.rec + j, s.split + j
                        tile = s.tile + j * len(s.gates)
                        c = cell_c[:, layer, j, :]
                        i_gate, f_gate, g_gate, o_gate = (gates[:, layer, j, g, :] for g in range(4))
                        if layer == 0:
                            if s.first:
                                dve.wait_ge(emb_gates_put, s.batch * M + EMB_BEFORE[j + 1])
                            elif s.opens_f:
                                dve.wait_ge(emb_gates_put, (s.batch + 1) * M)
                            for g in s.gates[0:-1]:
                                add_embeddings(s, j, g)
                        dve.wait_ge(gate_act[layer], tile + 2)
                        if s.first:
                            nc.vector.tensor_tensor(c, i_gate, g_gate, ALU.mult).then_inc(c_done[layer], 1)
                        else:
                            nc.vector.tensor_tensor(ig[:, j, :], i_gate, g_gate, ALU.mult).then_inc(ig_done[layer], 1)
                        if layer == 0:
                            add_embeddings(s, j, GATE_O)
                        if not s.first:
                            dve.wait_ge(gate_act[layer], tile + 3)
                            nc.vector.tensor_tensor(c, f_gate, c, ALU.mult).then_inc(fc_done[layer], 1)
                            dve.wait_ge(ig_done[layer], rec + 1)
                            dve.wait_ge(fc_done[layer], rec + 1)
                            nc.vector.tensor_tensor(c, c, ig[:, j, :], ALU.add).then_inc(c_done[layer], 1)
                        dve.wait_ge(gate_act[layer], tile + len(s.gates))
                        dve.wait_ge(tanh_c_done[layer], half + 1)
                        if s.last:
                            nc.vector.tensor_tensor(h_last[:, j, :], o_gate, tanh_c[:, layer, j, :], ALU.mult
                                                    ).then_inc(h_done[layer], 1)
                            continue
                        hi = h_part[:, layer, s.write_slot, HI, j, :]
                        lo = h_part[:, layer, s.write_slot, LO, j, :]
                        nc.vector.tensor_tensor(h_full[:, j, :], o_gate, tanh_c[:, layer, j, :], ALU.mult
                                                ).then_inc(h_full_done[layer], 1)
                        nc.vector.tensor_tensor(hi, o_gate, tanh_c[:, layer, j, :], ALU.mult
                                                ).then_inc(h_hi_done[layer], 1)
                        dve.wait_ge(h_full_done[layer], split + 1)
                        dve.wait_ge(h_hi_done[layer], split + 1)
                        nc.vector.tensor_tensor(lo, h_full[:, j, :], hi, ALU.subtract).then_inc(h_done[layer], 1)
                elif kind == "head":
                    n = stage[1]
                    for g in range(GR):
                        dve.wait_ge(y_acc, n * GR + g + 1)
                        nc.vector.tensor_tensor(y[:, g, :], aux[:, g, :], b_head[:, :], ALU.add
                                                ).then_inc(y_put, 1)
                    if not isinstance(n, int):
                        dve.wait_ge(y_out, (n + 1) * GR * DMA)

        @block.tensor
        def _(pe):
            pe.wait_ge(proj_in, (5 + TT) * DMA)
            for s in range(TT):
                for k in range(TAPS):
                    at = PAD - (s + k) * D_FEAT
                    mm = nc.tensor.matmul(aux[0:KF, 0, s * D_CONV:(s + 1) * D_CONV], proj_t[:, at:at + KF],
                                          conv_w[:, k, :], start=(k == 0), stop=(k == TAPS - 1))
            mm.then_inc(band_acc, 1)
            for s in range(TT):
                for k in range(TAPS):
                    mm = nc.tensor.matmul(aux[s * D_CONV:(s + 1) * D_CONV, 1, 0:1], conv_w[:, k, :],
                                          proj_bias[:, :], start=(k == 0), stop=(k == TAPS - 1))
            mm.then_inc(band_acc, 1)

            pe.wait_ge(poi_hot_ready, 4)
            hot = poi_hot[:, :].rearrange("k (p g t) -> k g t p", g=GR, t=T)
            for g in range(GR):
                for t in range(T):
                    at = (g * T + t) * 3 * D_POI
                    mm = nc.tensor.matmul(aux[:, 3, at:at + 3 * D_POI], hot[:, g, t, :],
                                          poi_part[:, :, :].rearrange("k s f -> k (s f)"), start=True, stop=True)
            mm.then_inc(poi_acc, 1)

            pe.wait_ge(ident_ready, 1)
            pe.wait_ge(w1_in, 2 * DMA)
            for k in range(D1 // P):
                for a in range(HK):
                    mm = nc.tensor.transpose(acc[:, k // 2, (k % 2 * HK + a) * P:(k % 2 * HK + a + 1) * P],
                                             w1_nat[:, a, k * P:(k + 1) * P], ident[:, :])
                if k % 2 == 1:
                    mm.then_inc(w1_turned, 1)
            pe.wait_ge(w1_put, 2)
            pe.wait_ge(w2_in, 2 * DMA)
            for m in range(D2 // P):
                if m >= 4:
                    pe.wait_ge(w12_put, 2 * (m - 3))
                for k in range(D1 // P):
                    mm = nc.tensor.matmul(acc[:, m % 4, 0:H + 1], w2[:, k, m * P:(m + 1) * P], w1_t[:, k, :],
                                          start=(k == 0), stop=(k == D1 // P - 1))
                mm.then_inc(w12_acc, 1)

            pe.wait_ge(wx_scaled, 1)
            for b in range(4):
                pe.wait_ge(w12_put, 2 * (D2 // P - 3 + b))
                rows, first_col = (3 * Q, 0) if b < 2 else (4 * Q, 3 * Q)
                for i in range(4):
                    mm = nc.tensor.transpose(acc[0:rows, b, i * P:(i + 1) * P],
                                             wx_nat[:, b % 2 * 4 + i, first_col:first_col + rows], ident[:, :])
                mm.then_inc(wx_turned, 1)

            pe.wait_ge(ident16_ready, 1)
            for i in range(3):
                for part, ready in ((HI, part_hi), (LO, part_lo)):
                    pe.wait_ge(ready, i + 1)
                    for k in range(HK):
                        b = 2 * HK * i + HK * part + k
                        if b == 0:
                            pe.wait_ge(band_put, 2)
                        elif b == 3:
                            pe.wait_ge(poi_put, 1)
                        elif b > 3:
                            pe.wait_ge(part_put, b - 3)
                        for m in range(M):
                            mm = nc.tensor.transpose(aux[:, b % 4, :].bitcast(F16)[:, m * P:(m + 1) * P],
                                                     w_part[:, part, m, k * P:(k + 1) * P], ident16[:, :])
                        mm.then_inc(part_turned, 1)
            pe.wait_ge(part_put, 12)

            for stage in stages(pe, NB, STEPS):
                kind = stage[0]
                if kind == "turn":
                    n, c = stage[1:]
                    pe.wait_ge(rows_in[c], rows_count(n, c))
                    pe.wait_ge(coords_put, n + 1)
                    if is_first(n):
                        if c == 0:
                            pe.wait_ge(poi_put, 1)
                        else:
                            pe.wait_ge(emb_gates_put, EMB_BEFORE[2])
                    for g in range(GR):
                        mm = nc.tensor.transpose(
                            aux[0:KF, c, g * P:(g + 1) * P],
                            feat[:, g, c * TT:c * TT + WIN, :].rearrange("p t f -> p (t f)"), ident[:, :])
                    mm.then_inc(turned[c], 1)
                elif kind == "turn_emb":
                    n = stage[1]
                    pe.wait_ge(emb_copied, n + 1)
                    for g in range(GR):
                        mm = nc.tensor.transpose(aux[:, 2, g * P:(g + 1) * P],
                                                 emb[:, g, :, :].rearrange("p q f -> p (q f)"), ident[:, :])
                    mm.then_inc(emb_turned, 1)
                elif kind == "emb_gates":
                    n, part = stage[1:]
                    if part == 0:
                        pe.wait_ge(emb_ready, (n + 1) * 2)
                        pe.wait_ge(turned_put[0], n + 1)
                        if not is_first(n):
                            pe.wait_ge(turned_put[1], n + 1)
                    else:
                        pe.wait_ge(emb_gates_put, n * M + EMB_BEFORE[part])
                    for j, g, bank in EMB_PARTS[part]:
                        m = g * HK + j
                        nc.tensor.matmul(aux[:, bank, :], we[:, m * P:(m + 1) * P], emb_in[:, :],
                                         start=True, stop=True).then_inc(emb_gates_acc, 1)
                elif kind == "conv":
                    n, c = stage[1:]
                    pe.wait_ge(turned_put[c], n + 1)
                    if c == 1:
                        pe.wait_ge(relu_done, n * CH + 1)
                        pe.wait_ge(neg_done, n * CH + 1)
                    nc.tensor.matmul(aux[:, 3, :], conv_band[:, :], feat_t[:, c, :], start=True, stop=True
                                     ).then_inc(conv_acc, 1)
                elif kind == "head_weights":
                    if stage[1] == 0:
                        pe.wait_ge(w3_in, 2 * DMA)
                        pe.wait_ge(wx_lo_put, 4)
                        for a in range(HK):
                            for k in range(D2 // P):
                                mm = nc.tensor.matmul(acc[:, a, :], w12_t[:, k, a * P:(a + 1) * P], w3[:, k, :],
                                                      start=(k == 0), stop=(k == D2 // P - 1))
                            mm.then_inc(head_acc, 1)
                    else:
                        for k in range(D2 // P):
                            mm = nc.tensor.matmul(acc[:, HK, :], w12_t[:, k, H:H + 1].to_broadcast([P, P]),
                                                  w3[:, k, :], start=(k == 0), stop=(k == D2 // P - 1))
                        mm.then_inc(head_acc, 1)
                elif kind == "cell":
                    s = stage[1]
                    layer = s.layer
                    own_w = 2 * layer
                    if s.before is None:
                        pe.wait_ge(head_put, HK + 1)
                    if s.x_part is not None:
                        pe.wait_ge(x_put[s.x_part], (s.batch + 1) * X_DMAS[s.x_part])
                    for j in range(HK):
                        for g in s.gates:
                            m = g * HK + j
                            rows = slice(m * P, (m + 1) * P)
                            bank = acc[:, s.bank(j, g), :]
                            place = s.place(j, g)
                            opens = place == 0
                            if place >= 4:
                                pe.wait_ge(acc_read[layer], s.tile + (place - 3))
                            elif s.before is not None:
                                before_layer, before_end = s.before
                                pe.wait_ge(acc_read[before_layer], before_end + (place - 3))
                            if layer == 0:
                                mm = nc.tensor.matmul(bank, wx[:, rows], x_in[:, s.t, :], start=True,
                                                      stop=s.first)
                            else:
                                for c in range(HK):
                                    if opens:
                                        pe.wait_ge(h_done[0], s.half + (c + 1))
                                    for a, b in ((HI, HI), (HI, LO), (LO, HI)):
                                        mm = nc.tensor.matmul(bank, wh[:, 1, a, c, rows],
                                                              h_part[:, 0, s.write_slot, b, c, :],
                                                              start=(c == 0 and a == b == HI),
                                                              stop=(s.first and c == HK - 1 and a == LO))
                            if not s.first:
                                for c in range(HK):
                                    if opens:
                                        pe.wait_ge(h_done[layer], s.half + (c - 1 + (ahead if layer == 1 else 0)))
                                    for a, b in ((HI, HI), (HI, LO), (LO, HI)):
                                        mm = nc.tensor.matmul(bank, wh[:, own_w, a, c, rows],
                                                              h_part[:, layer, s.read_slot, b, c, :],
                                                              start=False, stop=(c == HK - 1 and a == LO))
                            mm.then_inc(gate_acc[layer], 1)
                elif kind == "head":
                    n = stage[1]
                    pe.wait_ge(h_done[1], ahead + (n + 1) * 2 * STEPS)
                    for g in range(GR):
                        for c in range(HK):
                            mm = nc.tensor.matmul(aux[:, g, :], h_last[:, c, g * P:(g + 1) * P], w_head[:, c, :],
                                                  start=(c == 0), stop=(c == HK - 1))
                        mm.then_inc(y_acc, 1)


_PREFIX = "L0_rec_"
_OUT = (2048, 512)


def kernel(**inputs):
    import numpy as _np
    import concourse.bacc as _bacc
    from concourse import mybir as _mybir
    from concourse.bass_utils import run_bass_kernel_spmd as _run

    nc = _bacc.Bacc("TRN2", target_bir_lowering=False, num_devices=1)
    arrays, tensors = {}, {}
    for name, value in inputs.items():
        a = _np.ascontiguousarray(value)
        arrays[f"in_{name}"] = a
        tensors[name.replace(_PREFIX, "")] = nc.dram_tensor(f"in_{name}", a.shape, _mybir.dt.from_np(a.dtype),
                                                            kind="ExternalInput").ap()
    tensors["out"] = nc.dram_tensor("out_0", _OUT, _mybir.dt.from_np(_np.dtype("float32")),
                                    kind="ExternalOutput").ap()
    build(nc, tensors)
    return _run(nc, [arrays], core_ids=[0]).results[0]["out_0"]
```

```python
from contextlib import ExitStack

import concourse.bass as bass
from concourse import mybir

F32 = mybir.dt.float32
F32R = mybir.dt.float32r
F16 = mybir.dt.float16
BF16 = mybir.dt.bfloat16
I32 = mybir.dt.int32
ALU = mybir.AluOpType
ACT = mybir.ActivationFunctionType
AX = mybir.AxisListType

P = 128
NCOL = 512
GATE_I, GATE_F, GATE_G, GATE_O = range(4)
GATE_ORDER = (GATE_I, GATE_G, GATE_F, GATE_O)
HI, LO = 0, 1
DMA = 16

EXP_ONE = 1 << 23
EXP_MASK = 0x7F800000
EXP_LEAST = 121 * EXP_ONE
SCALE_FROM = (127 + 14 + 127) * EXP_ONE
UNSCALE_BY = 14 * EXP_ONE


class Cell:

    def __init__(self, layer, t, counts, bank0, before, slots=None, first=False, last=False, batch=None,
                 x_part=None):
        self.layer, self.t, self.first, self.last = layer, t, first, last
        self.batch, self.x_part = batch, x_part
        self.left = None
        self.leaves = False
        self.opens_f = layer == 0 and isinstance(t, int) and t == 1
        self.tile, self.half, self.rec, self.split = counts
        self.bank0 = bank0
        self.before = before
        self.read_slot, self.write_slot = slots if slots else ((t + 1) % 2, t % 2)
        self.gates = [g for g in GATE_ORDER if not (first and g == GATE_F)]

    def place(self, j, g):
        return j * len(self.gates) + self.gates.index(g)

    def bank(self, j, g):
        return (self.bank0 + self.place(j, g)) % 4


def stages(eng, nbatch, steps):
    snap = eng.snap
    last_t = steps - 1
    tiles, halves = 8 * steps - 2, 2 * steps

    class Base:

        def __init__(self, n):
            self.batch = n
            reg = (lambda v: v) if isinstance(n, int) else snap
            self.tiles, self.halves, self.recs = reg(n * tiles), reg(n * halves), reg(n * (halves - 2))

        def tile(self, t):
            return self.tiles + (8 * t - 2 if t else 0)

        def counts(self, layer, t):
            rec = self.recs + (2 * t - 2 if t else 0)
            return self.tile(t), self.halves + 2 * t, rec, (self.halves if layer == 0 else self.recs) + 2 * t

    def cell(base, layer, t, bank0, before):
        x_part = {(0, 0): 0, (0, 1): 1}.get((layer, t))
        return "cell", Cell(layer, t, base.counts(layer, t), bank0, before, first=(t == 0),
                            last=(layer == 1 and t == last_t), batch=base.batch, x_part=x_part)

    def body(n, following):
        base = Base(n)
        bank = 14 % 4
        yield cell(base, 1, 0, bank, (0, base.tile(2)))
        bank = (bank + 6) % 4
        with eng.Fori(0, steps - 4) as u:
            t = snap(u + 2)
            even, odd = snap(t % 2), snap((u + 1) % 2)
            tile, half = snap(base.tiles + u * 8 + 6), snap(base.halves + u * 2 + 2)
            rec = snap(base.recs + u * 2)
            yield "cell", Cell(0, t, (tile + 8, half + 2, rec + 2, half + 2), bank, (1, tile), slots=(odd, even),
                               batch=n, x_part=2)
            yield "cell", Cell(1, None, (tile, half, rec, rec + 2), bank, (0, tile + 16), slots=(even, odd))
        yield cell(base, 0, last_t - 1, bank, (1, base.tile(last_t - 2)))
        if following:
            yield "turn", n + 1, 0
            yield "turn", n + 1, 1
            yield "turn_emb", n + 1
        yield cell(base, 1, last_t - 2, bank, (0, base.tile(last_t)))
        yield cell(base, 0, last_t, bank, (1, base.tile(last_t - 1)))
        if following:
            yield "conv", n + 1, 0
            yield "emb_gates", n + 1, 0
        upper = cell(base, 1, last_t - 1, bank, (0, base.tiles + tiles))
        upper[1].leaves = following
        yield upper
        before = (0, base.tiles + tiles)
        if following:
            yield "emb_gates", n + 1, 1
            after = Base(n + 1)
            opening = cell(after, 0, 0, bank, (1, base.tile(last_t)))
            opening[1].left = upper[1]
            yield opening
            bank = (bank + 6) % 4
            before = (0, after.tile(1))
            yield "emb_gates", n + 1, 2
            yield "conv", n + 1, 1
            yield cell(base, 1, last_t, bank, before)
            yield cell(after, 0, 1, bank, (1, base.tiles + tiles))
        else:
            yield cell(base, 1, last_t, bank, (1, base.tile(last_t)))
        yield "head", n

    assert tiles * 2 % 4 == 0
    base = Base(0)
    yield ("wx",)
    yield "split", 0
    yield ("band",)
    yield "parts", 0
    yield ("w1",)
    yield "w12", 0
    yield ("scales",)
    yield ("poi",)
    yield "split", 1
    yield "w12", 1
    yield "turn", 0, 0
    yield "parts", 1
    yield "split", 2
    yield "conv", 0, 0
    yield "turn_emb", 0
    yield "head_weights", 0
    yield "parts", 2
    yield "emb_gates", 0, 0
    yield "emb_gates", 0, 1
    yield cell(base, 0, 0, 0, None)
    yield "turn", 0, 1
    yield "head_weights", 1
    yield "conv", 0, 1
    yield "head_weights", 2
    yield "emb_gates", 0, 2
    yield cell(base, 0, 1, 6 % 4, (0, base.tile(1)))
    yield ("set_up_done",)
    with eng.Fori(0, nbatch - 1) as n:
        yield from body(n, True)
    yield from body(nbatch - 1, False)


def build(nc, d):
    B, T, _ = d["r_coords"].shape
    REG, D_REG = d["region_tbl"].shape
    POI, D_POI = d["poi_tbl"].shape
    CAR, D_CAR = d["car_tbl"].shape
    WEEK, D_WEEK = d["week_tbl"].shape
    TIME, D_TIME = d["time_tbl"].shape
    D_RP = d["W_rp"].shape[1]
    D_CO = d["W_co"].shape[1]
    TAPS, D_NV, D_CONV = d["conv_w"].shape
    D_FEAT = D_REG + D_POI + 2
    D_EMB = D_CAR + D_WEEK + D_TIME
    D_X = D_CONV + D_EMB
    GATES, H = d["Whh0"].shape
    HK = H // P
    M = GATES // P
    D1, D2, D3 = d["W1"].shape[1], d["W2"].shape[1], d["W3"].shape[1]
    STEPS = T - TAPS + 1
    NB = B // NCOL
    GR = NCOL // P
    TT = P // D_CONV
    CH = STEPS // TT
    WIN = (TT + TAPS - 1)
    KF = WIN * D_FEAT
    Q = 32
    assert HK == 2 and M == 8 and CH == 2 and D_RP + D_CO == D_NV and D_CONV == Q and D_EMB <= Q
    assert POI & (POI - 1) == 0

    with ExitStack() as ctx:
        def sb(name, shape, dt, stack=ctx):
            return stack.enter_context(nc.sbuf_tensor(name, shape, dt))

        def sem(name):
            return ctx.enter_context(nc.semaphore(name))

        idx_raw = {"region": sb("region_raw", [P, NB * GR, T], I32), "poi": sb("poi_raw", [P, NB * GR, T], I32),
                   "car": sb("car_raw", [P, NB * GR, 1], I32), "week": sb("week_raw", [P, NB * GR, 1], I32),
                   "time": sb("time_raw", [P, NB * GR, 1], I32)}
        idx_wrap = sb("idx_wrap", [P, NB * GR, T], F32)
        idx = {k: sb(f"{k}_idx", list(v.shape), I32) for k, v in idx_raw.items()}
        coords = sb("coords", [P, NB * GR, T * 2], F32)
        feat = sb("feat", [P, GR, T, D_FEAT], F32)
        emb = sb("emb", [P, GR, 4, Q], F32)
        feat_t = sb("feat_t", [KF, CH, NCOL], F32)
        relu_part = sb("relu_part", [P, NCOL], F32)
        neg_part = sb("neg_part", [P, NCOL], F32)
        tanh_part = sb("tanh_part", [P, NCOL], F32)
        conv_hi = sb("conv_hi", [P, CH, NCOL], F32R)
        conv_lo = sb("conv_lo", [P, CH, NCOL], F32R)
        emb_tanh = sb("emb_tanh", [P, NCOL], F32)
        emb_in = sb("emb_in", [P, NCOL], F32R)
        wx = sb("wx", [3 * Q, GATES], F32R)
        we = sb("we", [P, GATES], F32R)
        wh = sb("wh", [P, 3, 2, HK, GATES], F16)
        w_head = sb("w_head", [P, 2, HK, D3], F32R)
        b_head = sb("b_head", [P, D3], F32)
        conv_band = sb("conv_band", [KF, P], F32)
        conv_bias = sb("conv_bias", [P, 1], F32)
        gate_bias = sb("gate_bias", [P, 2, M], F32)
        unscale = sb("unscale", [P, 2, M], F32)
        ident = sb("ident", [P, P], F32)
        ident16 = sb("ident16", [P, P], F16)
        before_first = sb("before_first", [P, 1], F32)

        with ExitStack() as early:
            poi_all = sb("poi_all", [POI, NCOL * T], I32, early)
            poi_hot = sb("poi_hot", [POI, NCOL * T], BF16, early)
        x_in = sb("x_in", [3 * Q, STEPS, NCOL], F32R)
        emb_gates = sb("emb_gates", [P, M, NCOL], F32)

        with ExitStack() as setup:
            w1_nat = sb("w1_nat", [P, HK, D1], F32, setup)
            w1_t = sb("w1_t", [P, D1 // P, H + 1], F32, setup)
            w2 = sb("w2", [P, D1 // P, D2], F32, setup)
            wx_nat = sb("wx_nat", [P, M, 7 * Q], F32, setup)
            w_nat = [sb("w_nat0", [P, M, H], F32, setup)]
            PAD = (WIN - 1) * D_FEAT
            proj_t = sb("proj_t", [D_NV, PAD + D_FEAT + PAD], F32, setup)
            conv_w = sb("conv_w", [D_NV, TAPS, D_CONV], F32, setup)
            proj_bias = sb("proj_bias", [D_NV, 1], F32, setup)
            conv_b = sb("conv_b", [P, 1], F32, setup)
            poi_sum = sb("poi_sum", [P, GR * T, D_POI], F32, setup)
            poi_tbl = sb("poi_tbl", [POI, D_POI], F32, setup)
            poi_rest = sb("poi_rest", [POI, 2, D_POI], F32, setup)
            poi_part = sb("poi_part", [POI, 3, D_POI], BF16, setup)
            poi_number = sb("poi_number", [POI, 1], F32, setup)
            b2_col = sb("b2_col", [P, D2 // P], F32, setup)
            w_part = sb("w_part", [P, 2, M, H], F16, setup)
            w_nat.extend(sb(f"w_nat{i}", [P, M, H], F32, setup) for i in (1, 2))
            w3 = sb("w3", [P, D2 // P, D3], F32, setup)
            w12_t = sb("w12_t", [P, D2 // P, H + 1], F32, setup)
            b3_row = sb("b3_row", [P, D3], F32, setup)
            bias_in = sb("bias_in", [P, 2, 2, M], F32, setup)
            row_max = sb("row_max", [P, 3, M], F32, setup)
            exp_bits = sb("exp_bits", [P, 2, M], I32, setup)
            row_scale = sb("row_scale", [P, 2, M], F32, setup)

        gates, cell_c, tanh_c, h_part = [], [], [], []
        for layer in range(2):
            gates.append(sb(f"gates{layer}", [P, HK, 4, NCOL], F32))
            cell_c.append(sb(f"cell_c{layer}", [P, HK, NCOL], F32))
            tanh_c.append(sb(f"tanh_c{layer}", [P, HK, NCOL], F32))
            h_part.append(sb(f"h_part{layer}", [P, 2, 2, HK, NCOL], F16))
            if layer == 0:
                h_full = sb("h_full", [P, HK, NCOL], F32)
                ig = sb("ig", [P, HK, NCOL], F32)
        h_last = sb("h_last", [P, 2, HK, NCOL], F32R)
        y = sb("y", [P, GR, D3], F32)

        acc = ctx.enter_context(nc.psum_tensor("acc", [P, 4, NCOL], F32))
        aux = ctx.enter_context(nc.psum_tensor("aux", [P, 4, NCOL], F32))

        idx_in = {k: sem(f"{k}_in") for k in idx_raw}
        coords_in = sem("coords_in")
        poi_all_in, poi_tbl_in = sem("poi_all_in"), sem("poi_tbl_in")
        w_in = [sem(f"w_in{i}") for i in range(3)]
        wx_in = sem("wx_in")
        bias_loaded = sem("bias_loaded")
        proj_in = sem("proj_in")
        w1_in, w2_in, w3_in = sem("w1_in"), sem("w2_in"), sem("w3_in")
        rows_in = [sem("rows0_in"), sem("rows1_in")]
        emb_rows_in = sem("emb_rows_in")
        zeroed = sem("zeroed")
        ident_zero, ident_ready, ident16_ready = sem("ident_zero"), sem("ident_ready"), sem("ident16_ready")
        idx_step, idx_ready = sem("idx_step"), sem("idx_ready")
        number_ready = sem("number_ready")
        poi_step, poi_hot_ready, poi_acc, poi_put = sem("poi_step"), sem("poi_hot_ready"), sem("poi_acc"), sem("poi_put")
        coords_put = sem("coords_put")
        emb_copied = sem("emb_copied")
        prep = sem("prep")
        bias_ready = sem("bias_ready")
        wx_scaled, scaled = sem("wx_scaled"), sem("scaled")
        part_hi, part_lo = sem("part_hi"), sem("part_lo")
        part_turned = sem("part_turned")
        part_put = sem("part_put")
        band_acc, band_put = sem("band_acc"), sem("band_put")
        wx_turned, wx_hi_put, wx_lo_put = sem("wx_turned"), sem("wx_hi_put"), sem("wx_lo_put")
        w1_turned, w1_put = sem("w1_turned"), sem("w1_put")
        w12_acc, w12_put = sem("w12_acc"), sem("w12_put")
        head_acc, head_put, head_low_put = sem("head_acc"), sem("head_put"), sem("head_low_put")
        turned, turned_put = [sem("turned0"), sem("turned1")], [sem("turned0_put"), sem("turned1_put")]
        emb_turned, emb_act, emb_step, emb_ready = sem("emb_turned"), sem("emb_act"), sem("emb_step"), sem("emb_ready")
        emb_gates_acc, emb_gates_put = sem("emb_gates_acc"), sem("emb_gates_put")
        conv_acc = sem("conv_acc")
        relu_done, neg_done, tanh_done = sem("relu_done"), sem("neg_done"), sem("tanh_done")
        elu_step, conv_hi_put, conv_lo_put = sem("elu_step"), sem("conv_hi_put"), sem("conv_lo_put")
        x_put = [sem("x0_put"), sem("x1_put"), sem("x2_put")]
        def both(name):
            return [sem(f"{name}{layer}") for layer in range(2)]

        gate_acc, gate_act = both("gate_acc"), both("gate_act")
        gate_sum = sem("gate_sum")
        ig_done, fc_done, c_done, tanh_c_done = both("ig_done"), both("fc_done"), both("c_done"), both("tanh_c_done")
        h_full_done, h_hi_done, h_done = both("h_full_done"), both("h_hi_done"), both("h_done")
        last_step = sem("last_step")
        y_acc, y_put, y_out = sem("y_acc"), sem("y_put"), sem("y_out")

        ahead = 2
        TABLES_FIRST, TABLES = 1, 2
        OWN_STEPS = (WIN, T - WIN)
        tables = {"region": d["region_tbl"], "poi": d["poi_tbl"], "car": d["car_tbl"],
                  "week": d["week_tbl"], "time": d["time_tbl"]}
        EMB_PARTS = [[(j, g, i) for i, g in enumerate((GATE_I, GATE_G, GATE_O))] for j in range(HK)]
        EMB_PARTS.append([(j, GATE_F, 2 * j) for j in range(HK)])
        EMB_BEFORE = (0, 3, 6)
        PART_BANKS = ((2, 3, 0, 1), (1, 2, 1, 2), (0, 1, 0, 1))
        W12_TILES = (range(D2 // P - 2), range(D2 // P - 2, D2 // P))
        HEAD_BANKS = (acc[:, 3, :], aux[:, 0, :], aux[:, 1, :])
        acc_read = (gate_sum, gate_act[1])
        X_DMAS = (3 * DMA, 3 * (TT - 1) * DMA, 3 * TT * DMA)

        def is_first(n):
            return isinstance(n, int) and n == 0

        def rows_count(n, c):
            return (n * TABLES + TABLES_FIRST) * GR * OWN_STEPS[c] * DMA

        block = ctx.enter_context(nc.Block())

        @block.sync
        def _(sp):
            def load(out, src, loaded):
                sp.dma_start(out, src, allow_slow_non_contiguous=True).then_inc(loaded, DMA)

            def load_rows(k):
                load(idx_raw[k][:, :, :].rearrange("p (n g) t -> p n g t", g=GR),
                     d[f"r_{k}_idx"].rearrange("(n p g) t -> p n g t", p=P, g=GR), idx_in[k])

            load_rows("region")
            load(w_nat[0][:, :, :], d["Whh0"].rearrange("(m p) k -> p m k", p=P), w_in[0])
            for k in ("car", "week", "time"):
                load(idx_raw[k][:, :, 0].rearrange("p (n g) -> p n g", g=GR),
                     d[f"r_{k}_idx"].rearrange("(n p g) -> p n g", p=P, g=GR), idx_in[k])
            sp.wait_ge(zeroed, 3)
            wih0 = d["Wih0"].rearrange("(m p) k -> p m k", p=P)
            for q in range(3):
                load(wx_nat[:, :, q * Q:q * Q + D_CONV], wih0[:, :, 0:D_CONV], wx_in)
            for q in range(3, 7):
                load(wx_nat[:, :, q * Q:q * Q + D_EMB], wih0[:, :, D_CONV:D_X], wx_in)
            load(proj_t[0:D_RP, PAD:PAD + D_REG + D_POI], d["W_rp"].rearrange("i o -> o i"), proj_in)
            load(proj_t[D_RP:D_NV, PAD + D_REG + D_POI:PAD + D_FEAT], d["W_co"].rearrange("i o -> o i"), proj_in)
            load(conv_w[:, :, :], d["conv_w"].rearrange("k i o -> i k o"), proj_in)
            load(proj_bias[0:D_RP, 0], d["b_rp"], proj_in)
            load(proj_bias[D_RP:D_NV, 0], d["b_co"], proj_in)
            for k in range(TT):
                load(conv_b[k * D_CONV:(k + 1) * D_CONV, 0], d["conv_b"], proj_in)
            load(w1_nat[:, :, :], d["W1"].rearrange("(a p) n -> p a n", p=P), w1_in)
            load(w1_t[:, :, H], d["b1"].rearrange("(k p) -> p k", p=P), w1_in)
            load(poi_all[:, :], d["r_poi_idx"][0:NCOL, :].rearrange("(a b) t -> a (b t)", a=1)
                 .partition_broadcast(POI)[:, 0, :], poi_all_in)
            load(poi_tbl[:, :], d["poi_tbl"], poi_tbl_in)
            load(w2[:, :, :], d["W2"].rearrange("(k p) n -> p k n", p=P), w2_in)
            load(b2_col[:, :], d["b2"].rearrange("(k p) -> p k", p=P), w2_in)
            load(coords[:, :, :].rearrange("p (n g) x -> p n g x", g=GR),
                 d["r_coords"].rearrange("(n p g) t c -> p n g (t c)", p=P, g=GR), coords_in)
            for layer in range(2):
                for i, k in enumerate(("bih", "bhh")):
                    load(bias_in[:, layer, i, :], d[f"{k}{layer}"].rearrange("(m p) -> p m", p=P), bias_loaded)
            for i, k in ((1, "Wih1"), (2, "Whh1")):
                load(w_nat[i][:, :, :], d[k].rearrange("(m p) k -> p m k", p=P), w_in[i])
            load(w3[:, :, :], d["W3"].rearrange("(k p) n -> p k n", p=P), w3_in)
            load(b3_row[:, :], d["b3"].rearrange("(a n) -> a n", a=1).partition_broadcast(P)[:, 0, :], w3_in)
            load_rows("poi")

            out_rows = d["out"].rearrange("(n p g) o -> p n g o", p=P, g=GR)
            for stage in stages(sp, NB, STEPS):
                kind = stage[0]
                if kind == "conv":
                    n, c = stage[1:]
                    sp.wait_ge(conv_hi_put, n * CH + c + 1)
                    sp.wait_ge(conv_lo_put, n * CH + c + 1)
                    for k in range(TT):
                        t = c * TT + k
                        put = x_put[0 if t == 0 else c + 1]
                        for q, part in enumerate((conv_hi, conv_lo, conv_hi)):
                            sp.dma_start(x_in[q * Q:(q + 1) * Q, t, :].bitcast(F32),
                                         part[k * D_CONV:(k + 1) * D_CONV, c, :].bitcast(F32)).then_inc(put, DMA)
                elif kind == "head":
                    n = stage[1]
                    for g in range(GR):
                        sp.wait_ge(y_put, n * GR + g + 1)
                        sp.dma_start(out_rows[:, n, g, :], y[:, g, :]).then_inc(y_out, DMA)
            sp.wait_ge(y_out, NB * GR * DMA)

        @block.gpsimd
        def _(pool):
            nc.gpsimd.memset(emb[:, :, 0, D_EMB:Q], 0.0).then_inc(zeroed, 1)
            nc.gpsimd.memset(wx_nat[:, :, 3 * Q:7 * Q].rearrange("p m (q k) -> p m q k", k=Q)[:, :, :, D_EMB:Q], 0.0
                             ).then_inc(zeroed, 1)
            nc.gpsimd.memset(proj_t[:, :], 0.0).then_inc(zeroed, 1)
            nc.gpsimd.memset(ident[:, :], 0.0).then_inc(ident_zero, 1)
            pool.wait_ge(ident_zero, 1)
            nc.gpsimd.affine_select(out=ident[:, :], in_=ident[:, :], compare_op=ALU.not_equal, fill=1.0,
                                    base=0, pattern=[[-1, P]], channel_multiplier=1).then_inc(ident_ready, 1)
            nc.gpsimd.iota(poi_number[:, :], pattern=[[0, 1]], base=0, channel_multiplier=1,
                           allow_small_or_imprecise_dtypes=True).then_inc(number_ready, 1)
            pool.wait_ge(zeroed, 3)

            for n in range(NB):
                if n:
                    for c in range(CH):
                        pool.wait_ge(turned[c], n)
                    pool.wait_ge(emb_turned, n)
                if n == 1:
                    pool.wait_ge(idx_ready, 5)

                def gather(k, out, g, t, landed):
                    pool.indirect_dma_start(out, None, tables[k],
                                            bass.IndirectOffsetOnAxis(ap=idx[k][:, n * GR + g, t:t + 1], axis=0)
                                            ).then_inc(landed, DMA)

                def gather_steps(c):
                    begin = 0 if c == 0 else OWN_STEPS[0]
                    for g in range(GR):
                        for t in range(begin, begin + OWN_STEPS[c]):
                            gather("region", feat[:, g, t, 0:D_REG], g, t, rows_in[c])
                            if n:
                                gather("poi", feat[:, g, t, D_REG:D_REG + D_POI], g, t, rows_in[c])

                if n == 0:
                    pool.wait_ge(idx_ready, 1)
                gather_steps(0)
                if n == 0:
                    pool.wait_ge(coords_in, DMA)
                nc.gpsimd.tensor_copy(feat[:, :, :, D_REG + D_POI:D_FEAT],
                                      coords[:, n * GR:(n + 1) * GR, :].rearrange("p g (t c) -> p g t c", c=2)
                                      ).then_inc(coords_put, 1)
                if n == 0:
                    pool.wait_ge(idx_ready, 4)
                for g in range(GR):
                    gather("car", emb[:, g, 0, 0:D_CAR], g, 0, emb_rows_in)
                    gather("week", emb[:, g, 0, D_CAR:D_CAR + D_WEEK], g, 0, emb_rows_in)
                    gather("time", emb[:, g, 0, D_CAR + D_WEEK:D_EMB], g, 0, emb_rows_in)
                pool.wait_ge(emb_rows_in, (n + 1) * 3 * GR * DMA)
                nc.gpsimd.tensor_copy(emb[:, :, 1:4, :], emb[:, :, 0, :].unsqueeze(2).to_broadcast([P, GR, 3, Q])
                                      ).then_inc(emb_copied, 1)
                gather_steps(1)

        @block.scalar
        def _(act):
            for stage in stages(act, NB, STEPS):
                kind = stage[0]
                if kind == "w1":
                    for b in range(2):
                        act.wait_ge(w1_turned, b + 1)
                        nc.scalar.copy(w1_t[:, 2 * b:2 * b + 2, 0:H],
                                       acc[:, b, :].rearrange("p (k a) -> p k a", k=2)).then_inc(w1_put, 1)
                elif kind == "wx":
                    for b in range(4):
                        act.wait_ge(wx_turned, b + 1)
                        out, rows = (wx, 3 * Q) if b < 2 else (we, 4 * Q)
                        nc.scalar.copy(out[0:rows, b % 2 * NCOL:(b % 2 + 1) * NCOL], acc[0:rows, (b + 2) % 4, :]
                                       ).then_inc(wx_hi_put, 1)
                elif kind == "w12":
                    act.wait_ge(w2_in, 2 * DMA)
                    for m in W12_TILES[stage[1]]:
                        act.wait_ge(w12_acc, m + 1)
                        nc.scalar.copy(w12_t[:, m, 0:H], acc[:, m % 4, 0:H]).then_inc(w12_put, 1)
                        nc.scalar.activation(w12_t[:, m, H:H + 1], acc[:, m % 4, H:H + 1], ACT.Identity,
                                             bias=b2_col[:, m:m + 1]).then_inc(w12_put, 1)
                elif kind == "split":
                    i = stage[1]
                    act.wait_ge(scaled, i + 1)
                    if i:
                        act.wait_ge(part_turned, 2 * HK * i)
                    nc.scalar.copy(w_part[:, HI, :, :], w_nat[i][:, :, :]).then_inc(part_hi, 1)
                elif kind == "parts":
                    i = stage[1]
                    for part in (HI, LO):
                        for k in range(HK):
                            b = HK * part + k
                            act.wait_ge(part_turned, 2 * HK * i + b + 1)
                            nc.scalar.copy(wh[:, i, part, k, :], aux[:, PART_BANKS[i][b], :].bitcast(F16)
                                           ).then_inc(part_put, 1)
                elif kind == "head_weights" and stage[1] < HK:
                    a = stage[1]
                    act.wait_ge(head_acc, a + 1)
                    nc.scalar.copy(w_head[:, HI, a, :], HEAD_BANKS[a]).then_inc(head_put, 1)
                elif kind == "turn":
                    n, c = stage[1:]
                    act.wait_ge(turned[c], n + 1)
                    nc.scalar.copy(feat_t[:, c, :], aux[0:KF, c, :]).then_inc(turned_put[c], 1)
                elif kind == "turn_emb":
                    n = stage[1]
                    act.wait_ge(emb_turned, n + 1)
                    if not is_first(n):
                        act.wait_ge(emb_ready, n * 2)
                    nc.scalar.activation(emb_tanh[:, :], aux[:, 2, :], ACT.Tanh).then_inc(emb_act, 1)
                elif kind == "emb_gates":
                    n, part = stage[1:]
                    for i, (j, g, bank) in enumerate(EMB_PARTS[part]):
                        act.wait_ge(emb_gates_acc, n * M + EMB_BEFORE[part] + i + 1)
                        nc.scalar.copy(emb_gates[:, g * HK + j, :], aux[:, bank, :]).then_inc(emb_gates_put, 1)
                elif kind == "conv":
                    n, c = stage[1:]
                    chunk = n * CH + c
                    act.wait_ge(conv_acc, chunk + 1)
                    if is_first(n) and c == 0:
                        act.wait_ge(band_put, 2)
                    else:
                        act.wait_ge(conv_lo_put, chunk)
                    nc.scalar.activation(relu_part[:, :], aux[:, 3, :], ACT.Relu,
                                         bias=conv_bias[:, 0:1]).then_inc(relu_done, 1)
                    act.wait_ge(neg_done, chunk + 1)
                    nc.scalar.activation(tanh_part[:, :], neg_part[:, :], ACT.Tanh, scale=0.5
                                         ).then_inc(tanh_done, 1)
                elif kind == "cell":
                    s = stage[1]
                    layer = s.layer
                    if s.before is None:
                        act.wait_ge(prep, 5)
                        act.wait_ge(bias_ready, 1)
                    for j in range(HK):
                        if layer == 1:
                            act.wait_ge(h_done[1], ahead + s.half + j - 1)
                        for g in s.gates:
                            count = s.tile + s.place(j, g) + 1
                            if layer == 0:
                                act.wait_ge(gate_sum, count)
                                source = gates[0][:, j, g, :]
                            else:
                                act.wait_ge(gate_acc[1], count)
                                source = acc[:, s.bank(j, g), :]
                            m = g * HK + j
                            nc.scalar.activation(gates[layer][:, j, g, :], source,
                                                 ACT.Tanh if g == GATE_G else ACT.Sigmoid,
                                                 bias=gate_bias[:, layer, m:m + 1],
                                                 scale=unscale[:, layer, m:m + 1]).then_inc(gate_act[layer], 1)
                        act.wait_ge(c_done[layer], s.half + j + 1)
                        nc.scalar.activation(tanh_c[layer][:, j, :], cell_c[layer][:, j, :], ACT.Tanh
                                             ).then_inc(tanh_c_done[layer], 1)
                elif kind == "set_up_done":
                    act.wait_ge(prep, 12)

        @block.vector
        def _(dve):
            nc.vector.memset(before_first[:, :], 0.0).then_inc(h_done[1], ahead)
            def indices(i, k, rows):
                dve.wait_ge(idx_in[k], DMA)
                raw = idx_raw[k]
                wrap = idx_wrap[:, :, 0:raw.shape[2]]
                if i:
                    dve.wait_ge(idx_ready, i)
                nc.vector.tensor_scalar(wrap, raw[:, :, :], 0.0, float(rows), ALU.is_lt, ALU.mult
                                        ).then_inc(idx_step, 1)
                dve.wait_ge(idx_step, 2 * i + 1)
                nc.vector.tensor_tensor(wrap, wrap, raw[:, :, :], ALU.add).then_inc(idx_step, 1)
                dve.wait_ge(idx_step, 2 * i + 2)
                nc.vector.tensor_scalar(idx[k][:, :, :], wrap, 0.0, float(rows - 1), ALU.max, ALU.min
                                        ).then_inc(idx_ready, 1)

            indices(0, "region", REG)
            indices(1, "car", CAR)
            indices(2, "week", WEEK)
            indices(3, "time", TIME)

            dve.wait_ge(ident_ready, 1)
            nc.vector.tensor_copy(ident16[:, :], ident[:, :]).then_inc(ident16_ready, 1)

            def row_scales(layer, matrices, steps):
                for i in matrices:
                    dve.wait_ge(w_in[i], DMA)
                    nc.vector.tensor_reduce(row_max[:, i, :], w_nat[i][:, :, :], AX.X, ALU.max,
                                            apply_absolute_value=True).then_inc(prep, 1)
                steps += len(matrices)
                dve.wait_ge(prep, steps)
                if len(matrices) == 2:
                    nc.vector.tensor_tensor(row_max[:, 1, :], row_max[:, 1, :], row_max[:, 2, :], ALU.max
                                            ).then_inc(prep, 1)
                    steps += 1
                    dve.wait_ge(prep, steps)
                bits = exp_bits[:, layer, :]
                nc.vector.tensor_scalar(bits, row_max[:, layer, :].bitcast(I32), EXP_MASK, None,
                                        ALU.bitwise_and).then_inc(prep, 1)
                dve.wait_ge(prep, steps + 1)
                nc.vector.tensor_scalar(bits, bits, float(EXP_LEAST), None, ALU.max).then_inc(prep, 1)
                dve.wait_ge(prep, steps + 2)
                nc.vector.tensor_scalar(row_scale[:, layer, :].bitcast(I32), bits, -1.0, float(SCALE_FROM),
                                        ALU.mult, ALU.add).then_inc(prep, 1)
                nc.vector.tensor_scalar(unscale[:, layer, :].bitcast(I32), bits, float(-UNSCALE_BY), None,
                                        ALU.add).then_inc(prep, 1)
                dve.wait_ge(prep, steps + 4)

            def scale_weights(i):
                layer = 0 if i == 0 else 1
                nc.vector.tensor_tensor(w_nat[i][:, :, :], w_nat[i][:, :, :],
                                        row_scale[:, layer, :].unsqueeze(2).to_broadcast([P, M, H]), ALU.mult
                                        ).then_inc(scaled, 1)

            def low_parts(i):
                dve.wait_ge(part_hi, i + 1)
                nc.vector.tensor_tensor(w_part[:, LO, :, :], w_nat[i][:, :, :], w_part[:, HI, :, :], ALU.subtract
                                        ).then_inc(part_lo, 1)

            row_scales(0, (0,), 0)
            scale_weights(0)

            def poi_one_hot():
                dve.wait_ge(poi_all_in, DMA)
                nc.vector.tensor_scalar(poi_all[:, :], poi_all[:, :], float(-POI), float(POI - 1), ALU.max, ALU.min
                                        ).then_inc(poi_step, 1)
                dve.wait_ge(poi_step, 1)
                nc.vector.tensor_scalar(poi_all[:, :], poi_all[:, :], POI - 1, None, ALU.bitwise_and
                                        ).then_inc(poi_step, 1)
                dve.wait_ge(poi_step, 2)
                dve.wait_ge(number_ready, 1)
                nc.vector.tensor_scalar(poi_hot[:, :], poi_all[:, :], poi_number[:, 0:1], None, ALU.is_equal
                                        ).then_inc(poi_hot_ready, 1)
                dve.wait_ge(poi_tbl_in, DMA)
                rest = poi_tbl
                for k in range(3):
                    nc.vector.tensor_copy(poi_part[:, k, :], rest[:, :] if k == 0 else poi_rest[:, k - 1, :]
                                          ).then_inc(poi_hot_ready, 1)
                    if k < 2:
                        dve.wait_ge(poi_hot_ready, k + 2)
                        nc.vector.tensor_tensor(poi_rest[:, k, :], rest[:, :] if k == 0 else poi_rest[:, k - 1, :],
                                                poi_part[:, k, :], ALU.subtract).then_inc(poi_step, 1)
                        dve.wait_ge(poi_step, k + 3)

            def add_embeddings(s, j, g):
                dve.wait_ge(gate_acc[0], s.tile + s.place(j, g) + 1)
                nc.vector.tensor_tensor(gates[0][:, j, g, :], acc[:, s.bank(j, g), :], emb_gates[:, g * HK + j, :],
                                        ALU.add).then_inc(gate_sum, 1)

            def sums(s, layer, j):
                dve.wait_ge(emb_gates_put, s.batch * M + EMB_BEFORE[j + 1])
                for g in s.gates:
                    add_embeddings(s, j, g)

            def update_c(s, layer, j):
                tile = s.tile + j * len(s.gates)
                c = cell_c[layer][:, j, :]
                i_gate, f_gate, g_gate = (gates[layer][:, j, g, :] for g in (GATE_I, GATE_F, GATE_G))
                if layer == 0 and not s.first:
                    if s.opens_f:
                        dve.wait_ge(emb_gates_put, (s.batch + 1) * M)
                    for g in s.gates[0:-1]:
                        add_embeddings(s, j, g)
                dve.wait_ge(gate_act[layer], tile + 2)
                if s.first:
                    nc.vector.tensor_tensor(c, i_gate, g_gate, ALU.mult).then_inc(c_done[layer], 1)
                else:
                    nc.vector.tensor_tensor(ig[:, j, :], i_gate, g_gate, ALU.mult).then_inc(ig_done[layer], 1)
                if not s.first:
                    if layer == 0:
                        add_embeddings(s, j, GATE_O)
                    dve.wait_ge(gate_act[layer], tile + 3)
                    nc.vector.tensor_tensor(c, f_gate, c, ALU.mult).then_inc(fc_done[layer], 1)
                    dve.wait_ge(ig_done[layer], s.rec + (j + 1))
                    dve.wait_ge(fc_done[layer], s.rec + (j + 1))
                    nc.vector.tensor_tensor(c, c, ig[:, j, :], ALU.add).then_inc(c_done[layer], 1)

            def update_h(s, layer, j):
                split = s.split + j
                o_gate, th = gates[layer][:, j, GATE_O, :], tanh_c[layer][:, j, :]
                dve.wait_ge(gate_act[layer], s.tile + (j + 1) * len(s.gates))
                dve.wait_ge(tanh_c_done[layer], s.half + (j + 1))
                if s.last:
                    last = s.batch * HK + j
                    nc.vector.tensor_tensor(h_full[:, j, :], o_gate, th, ALU.mult).then_inc(last_step, 1)
                    dve.wait_ge(last_step, last * 2 + 1)
                    nc.vector.tensor_copy(h_last[:, HI, j, :], h_full[:, j, :]).then_inc(last_step, 1)
                    dve.wait_ge(last_step, last * 2 + 2)
                    nc.vector.tensor_tensor(h_last[:, LO, j, :], h_full[:, j, :], h_last[:, HI, j, :].bitcast(F32),
                                            ALU.subtract).then_inc(h_done[layer], 1)
                    return
                hi = h_part[layer][:, s.write_slot, HI, j, :]
                lo = h_part[layer][:, s.write_slot, LO, j, :]
                nc.vector.tensor_tensor(h_full[:, j, :], o_gate, th, ALU.mult).then_inc(h_full_done[layer], 1)
                nc.vector.tensor_tensor(hi, o_gate, th, ALU.mult).then_inc(h_hi_done[layer], 1)
                dve.wait_ge(h_full_done[layer], split + 1)
                dve.wait_ge(h_hi_done[layer], split + 1)
                nc.vector.tensor_tensor(lo, h_full[:, j, :], hi, ALU.subtract).then_inc(h_done[layer], 1)

            for stage in stages(dve, NB, STEPS):
                kind = stage[0]
                if kind == "wx":
                    dve.wait_ge(wx_in, 7 * DMA)
                    nc.vector.tensor_tensor(wx_nat[:, :, :], wx_nat[:, :, :],
                                            row_scale[:, 0, :].unsqueeze(2).to_broadcast([P, M, 7 * Q]), ALU.mult
                                            ).then_inc(wx_scaled, 1)
                    for b in range(4):
                        out, rows = (wx, 3 * Q) if b < 2 else (we, 4 * Q)
                        cols = slice(b % 2 * NCOL, (b % 2 + 1) * NCOL)
                        bank = (b + 2) % 4
                        dve.wait_ge(wx_hi_put, b + 1)
                        nc.vector.tensor_tensor(out[2 * Q:rows, cols], acc[2 * Q:rows, bank, :],
                                                out[2 * Q:rows, cols].bitcast(F32), ALU.subtract
                                                ).then_inc(wx_lo_put, 1)
                elif kind == "split":
                    low_parts(stage[1])
                elif kind == "parts":
                    i = stage[1]
                    if i == 0:
                        poi_one_hot()
                    if i == 2:
                        indices(4, "poi", POI)
                elif kind == "band":
                    dve.wait_ge(band_acc, 2)
                    nc.vector.tensor_copy(conv_band[:, :], aux[0:KF, 0, 0:P]).then_inc(band_put, 1)
                    nc.vector.tensor_tensor(conv_bias[:, :], aux[:, 1, 0:1], conv_b[:, :], ALU.add).then_inc(band_put, 1)
                elif kind == "poi":
                    dve.wait_ge(poi_acc, 1)
                    part_rows = aux[:, 3, 0:GR * T * 3 * D_POI].rearrange("p (r s) -> p r s", s=3 * D_POI)
                    nc.vector.tensor_copy(poi_sum[:, :, :], part_rows[:, :, 2 * D_POI:3 * D_POI]
                                          ).then_inc(poi_step, 1)
                    dve.wait_ge(poi_step, 5)
                    nc.vector.tensor_tensor(poi_sum[:, :, :], poi_sum[:, :, :], part_rows[:, :, D_POI:2 * D_POI],
                                            ALU.add).then_inc(poi_step, 1)
                    dve.wait_ge(poi_step, 6)
                    nc.vector.tensor_tensor(feat[:, :, :, D_REG:D_REG + D_POI],
                                            poi_sum[:, :, :].rearrange("p (g t) f -> p g t f", g=GR),
                                            part_rows[:, :, 0:D_POI].rearrange("p (g t) f -> p g t f", g=GR),
                                            ALU.add).then_inc(poi_put, 1)
                elif kind == "scales":
                    row_scales(1, (1, 2), 5)
                    scale_weights(1)
                    scale_weights(2)
                    dve.wait_ge(bias_loaded, 4 * DMA)
                    nc.vector.tensor_tensor(gate_bias[:, :, :], bias_in[:, :, 0, :], bias_in[:, :, 1, :],
                                            ALU.add).then_inc(bias_ready, 1)
                elif kind == "turn_emb":
                    n = stage[1]
                    dve.wait_ge(emb_act, n + 1)
                    nc.vector.tensor_copy(emb_in[:, :], emb_tanh[:, :]).then_inc(emb_step, 1)
                    dve.wait_ge(emb_step, n + 1)
                    for q in (1, 3):
                        rows = slice(q * Q, (q + 1) * Q)
                        nc.vector.tensor_tensor(emb_in[rows, :], emb_tanh[rows, :], emb_in[rows, :].bitcast(F32),
                                                ALU.subtract).then_inc(emb_ready, 1)
                elif kind == "conv":
                    n, c = stage[1:]
                    chunk = n * CH + c
                    dve.wait_ge(relu_done, chunk + 1)
                    nc.vector.tensor_scalar(neg_part[:, :], aux[:, 3, :], conv_bias[:, 0:1], 0.0,
                                            ALU.add, ALU.min).then_inc(neg_done, 1)
                    dve.wait_ge(tanh_done, chunk + 1)
                    nc.vector.tensor_scalar(neg_part[:, :], tanh_part[:, :], -1.0, 1.0, ALU.mult, ALU.add
                                            ).then_inc(elu_step, 1)
                    dve.wait_ge(elu_step, chunk * 4 + 1)
                    nc.vector.reciprocal(neg_part[:, :], neg_part[:, :]).then_inc(elu_step, 1)
                    dve.wait_ge(elu_step, chunk * 4 + 2)
                    nc.vector.scalar_tensor_tensor(neg_part[:, :], tanh_part[:, :], 2.0, neg_part[:, :],
                                                   ALU.mult, ALU.mult).then_inc(elu_step, 1)
                    dve.wait_ge(elu_step, chunk * 4 + 3)
                    nc.vector.tensor_tensor(relu_part[:, :], relu_part[:, :], neg_part[:, :], ALU.add
                                            ).then_inc(elu_step, 1)
                    dve.wait_ge(elu_step, chunk * 4 + 4)
                    if not is_first(n):
                        for i in ((0, 1) if c == 0 else (2,)):
                            dve.wait_ge(x_put[i], n * X_DMAS[i])
                    nc.vector.tensor_copy(conv_hi[:, c, :], relu_part[:, :]).then_inc(conv_hi_put, 1)
                    dve.wait_ge(conv_hi_put, chunk + 1)
                    nc.vector.tensor_tensor(conv_lo[:, c, :], relu_part[:, :], conv_hi[:, c, :].bitcast(F32),
                                            ALU.subtract).then_inc(conv_lo_put, 1)
                elif kind == "head_weights" and stage[1] < HK:
                    a = stage[1]
                    dve.wait_ge(head_put, a + 1)
                    nc.vector.tensor_tensor(w_head[:, LO, a, :], HEAD_BANKS[a], w_head[:, HI, a, :].bitcast(F32),
                                            ALU.subtract).then_inc(head_low_put, 1)
                elif kind == "head_weights" and stage[1] == HK:
                    dve.wait_ge(head_acc, HK + 1)
                    dve.wait_ge(w3_in, 2 * DMA)
                    nc.vector.tensor_tensor(b_head[:, :], HEAD_BANKS[HK], b3_row[:, :], ALU.add).then_inc(head_put, 1)
                elif kind == "cell":
                    s = stage[1]
                    layer = s.layer
                    if s.first and layer == 0:
                        sums(s, layer, 0)
                        if s.left is not None:
                            update_h(s.left, 1, 1)
                        update_c(s, layer, 0)
                        sums(s, layer, 1)
                        update_c(s, layer, 1)
                        update_h(s, layer, 0)
                        update_h(s, layer, 1)
                    elif layer == 0:
                        update_c(s, layer, 0)
                        update_c(s, layer, 1)
                        update_h(s, layer, 0)
                        update_h(s, layer, 1)
                    else:
                        update_c(s, layer, 0)
                        update_h(s, layer, 0)
                        update_c(s, layer, 1)
                        if not s.leaves:
                            update_h(s, layer, 1)
                elif kind == "head":
                    n = stage[1]
                    for g in range(GR):
                        dve.wait_ge(y_acc, n * GR + g + 1)
                        nc.vector.tensor_tensor(y[:, g, :], aux[:, g, :], b_head[:, :], ALU.add
                                                ).then_inc(y_put, 1)
                    if not isinstance(n, int):
                        dve.wait_ge(y_out, (n + 1) * GR * DMA)

        @block.tensor
        def _(pe):
            pe.wait_ge(ident_ready, 1)

            for stage in stages(pe, NB, STEPS):
                kind = stage[0]
                if kind == "w1":
                    pe.wait_ge(w1_in, 2 * DMA)
                    pe.wait_ge(wx_lo_put, 4)
                    for k in range(D1 // P):
                        for a in range(HK):
                            mm = nc.tensor.transpose(acc[:, k // 2, (k % 2 * HK + a) * P:(k % 2 * HK + a + 1) * P],
                                                     w1_nat[:, a, k * P:(k + 1) * P], ident[:, :])
                        if k % 2 == 1:
                            mm.then_inc(w1_turned, 1)
                elif kind == "wx":
                    pe.wait_ge(wx_scaled, 1)
                    for b in range(4):
                        rows, first_col = (3 * Q, 0) if b < 2 else (4 * Q, 3 * Q)
                        for i in range(4):
                            mm = nc.tensor.transpose(acc[0:rows, (b + 2) % 4, i * P:(i + 1) * P],
                                                     wx_nat[:, b % 2 * 4 + i, first_col:first_col + rows],
                                                     ident[:, :])
                        mm.then_inc(wx_turned, 1)
                elif kind == "parts":
                    i = stage[1]
                    pe.wait_ge(ident16_ready, 1)
                    if i == 1:
                        pe.wait_ge(part_put, 2 * HK)
                    elif i == 2:
                        pe.wait_ge(turned_put[0], 1)
                        pe.wait_ge(part_put, 4 * HK)
                    for part, ready in ((HI, part_hi), (LO, part_lo)):
                        pe.wait_ge(ready, i + 1)
                        for k in range(HK):
                            b = HK * part + k
                            if i == 0 and b == 2:
                                pe.wait_ge(band_put, 2)
                            elif i and b >= 2:
                                pe.wait_ge(part_put, 2 * HK * i + b - 1)
                            for m in range(M):
                                mm = nc.tensor.transpose(
                                    aux[:, PART_BANKS[i][b], :].bitcast(F16)[:, m * P:(m + 1) * P],
                                    w_part[:, part, m, k * P:(k + 1) * P], ident16[:, :])
                            mm.then_inc(part_turned, 1)
                elif kind == "band":
                    pe.wait_ge(proj_in, (5 + TT) * DMA)
                    for s in range(TT):
                        for k in range(TAPS):
                            at = PAD - (s + k) * D_FEAT
                            mm = nc.tensor.matmul(aux[0:KF, 0, s * D_CONV:(s + 1) * D_CONV], proj_t[:, at:at + KF],
                                                  conv_w[:, k, :], start=(k == 0), stop=(k == TAPS - 1))
                    mm.then_inc(band_acc, 1)
                    for s in range(TT):
                        for k in range(TAPS):
                            mm = nc.tensor.matmul(aux[s * D_CONV:(s + 1) * D_CONV, 1, 0:1], conv_w[:, k, :],
                                                  proj_bias[:, :], start=(k == 0), stop=(k == TAPS - 1))
                    mm.then_inc(band_acc, 1)
                elif kind == "poi":
                    pe.wait_ge(part_put, 2 * HK)
                    pe.wait_ge(poi_hot_ready, 4)
                    hot = poi_hot[:, :].rearrange("k (p g t) -> k g t p", g=GR, t=T)
                    for g in range(GR):
                        for t in range(T):
                            at = (g * T + t) * 3 * D_POI
                            mm = nc.tensor.matmul(aux[:, 3, at:at + 3 * D_POI], hot[:, g, t, :],
                                                  poi_part[:, :, :].rearrange("k s f -> k (s f)"), start=True, stop=True)
                    mm.then_inc(poi_acc, 1)
                elif kind == "w12":
                    pe.wait_ge(w1_put, 2)
                    pe.wait_ge(w2_in, 2 * DMA)
                    for m in W12_TILES[stage[1]]:
                        if m >= 4:
                            pe.wait_ge(w12_put, 2 * (m - 3))
                        for k in range(D1 // P):
                            mm = nc.tensor.matmul(acc[:, m % 4, 0:H + 1], w2[:, k, m * P:(m + 1) * P],
                                                  w1_t[:, k, :], start=(k == 0), stop=(k == D1 // P - 1))
                        mm.then_inc(w12_acc, 1)
                elif kind == "turn":
                    n, c = stage[1:]
                    pe.wait_ge(rows_in[c], rows_count(n, c))
                    pe.wait_ge(coords_put, n + 1)
                    if is_first(n):
                        if c == 0:
                            pe.wait_ge(poi_put, 1)
                            pe.wait_ge(part_put, 2 * HK)
                        else:
                            pe.wait_ge(emb_gates_put, EMB_BEFORE[2])
                    for g in range(GR):
                        mm = nc.tensor.transpose(
                            aux[0:KF, c, g * P:(g + 1) * P],
                            feat[:, g, c * TT:c * TT + WIN, :].rearrange("p t f -> p (t f)"), ident[:, :])
                    mm.then_inc(turned[c], 1)
                elif kind == "turn_emb":
                    n = stage[1]
                    pe.wait_ge(emb_copied, n + 1)
                    if is_first(n):
                        pe.wait_ge(part_put, 4 * HK)
                    for g in range(GR):
                        mm = nc.tensor.transpose(aux[:, 2, g * P:(g + 1) * P],
                                                 emb[:, g, :, :].rearrange("p q f -> p (q f)"), ident[:, :])
                    mm.then_inc(emb_turned, 1)
                elif kind == "emb_gates":
                    n, part = stage[1:]
                    if part == 0:
                        pe.wait_ge(emb_ready, (n + 1) * 2)
                        pe.wait_ge(turned_put[0], n + 1)
                        if is_first(n):
                            pe.wait_ge(part_put, 6 * HK)
                        else:
                            pe.wait_ge(turned_put[1], n + 1)
                    else:
                        pe.wait_ge(emb_gates_put, n * M + EMB_BEFORE[part])
                        if is_first(n) and part == 2:
                            pe.wait_ge(head_low_put, 2)
                    for j, g, bank in EMB_PARTS[part]:
                        m = g * HK + j
                        nc.tensor.matmul(aux[:, bank, :], we[:, m * P:(m + 1) * P], emb_in[:, :],
                                         start=True, stop=True).then_inc(emb_gates_acc, 1)
                elif kind == "conv":
                    n, c = stage[1:]
                    pe.wait_ge(turned_put[c], n + 1)
                    if c == 1:
                        pe.wait_ge(relu_done, n * CH + 1)
                        pe.wait_ge(neg_done, n * CH + 1)
                    nc.tensor.matmul(aux[:, 3, :], conv_band[:, :], feat_t[:, c, :], start=True, stop=True
                                     ).then_inc(conv_acc, 1)
                elif kind == "head_weights":
                    a = stage[1]
                    if a == 0:
                        pe.wait_ge(w3_in, 2 * DMA)
                        pe.wait_ge(w12_put, 2 * D2 // P)
                    elif a == 1:
                        pe.wait_ge(emb_gates_put, EMB_BEFORE[2])
                    else:
                        pe.wait_ge(turned_put[1], 1)
                    for k in range(D2 // P):
                        lhs = w12_t[:, k, a * P:(a + 1) * P] if a < HK else w12_t[:, k, H:H + 1].to_broadcast([P, P])
                        mm = nc.tensor.matmul(HEAD_BANKS[a], lhs, w3[:, k, :], start=(k == 0), stop=(k == D2 // P - 1))
                    mm.then_inc(head_acc, 1)
                elif kind == "set_up_done":
                    pe.wait_ge(head_put, HK + 1)
                elif kind == "cell":
                    s = stage[1]
                    layer = s.layer
                    own_w = 2 * layer
                    if s.before is None:
                        pe.wait_ge(head_low_put, 1)
                    if s.x_part is not None:
                        pe.wait_ge(x_put[s.x_part], (s.batch + 1) * X_DMAS[s.x_part])
                    for j in range(HK):
                        for g in s.gates:
                            m = g * HK + j
                            rows = slice(m * P, (m + 1) * P)
                            bank = acc[:, s.bank(j, g), :]
                            place = s.place(j, g)
                            opens = place == 0
                            if place >= 4:
                                pe.wait_ge(acc_read[layer], s.tile + (place - 3))
                            elif s.before is not None:
                                before_layer, before_end = s.before
                                pe.wait_ge(acc_read[before_layer], before_end + (place - 3))
                            if layer == 0:
                                mm = nc.tensor.matmul(bank, wx[:, rows], x_in[:, s.t, :], start=True,
                                                      stop=s.first)
                            else:
                                for c in range(HK):
                                    if opens:
                                        pe.wait_ge(h_done[0], s.half + (c + 1))
                                    for a, b in ((HI, HI), (HI, LO), (LO, HI)):
                                        mm = nc.tensor.matmul(bank, wh[:, 1, a, c, rows],
                                                              h_part[0][:, s.write_slot, b, c, :],
                                                              start=(c == 0 and a == b == HI),
                                                              stop=(s.first and c == HK - 1 and a == LO))
                            if not s.first:
                                for c in range(HK):
                                    if opens:
                                        pe.wait_ge(h_done[layer], s.half + (c - 1 + (ahead if layer == 1 else 0)))
                                    for a, b in ((HI, HI), (HI, LO), (LO, HI)):
                                        mm = nc.tensor.matmul(bank, wh[:, own_w, a, c, rows],
                                                              h_part[layer][:, s.read_slot, b, c, :],
                                                              start=False, stop=(c == HK - 1 and a == LO))
                            mm.then_inc(gate_acc[layer], 1)
                elif kind == "head":
                    n = stage[1]
                    for c in range(HK):
                        pe.wait_ge(h_done[1], n * (HK * STEPS) + (ahead + HK * STEPS + c - 1))
                        for g in range(GR):
                            for a, b in ((HI, HI), (HI, LO), (LO, HI)):
                                mm = nc.tensor.matmul(aux[:, g, :], h_last[:, a, c, g * P:(g + 1) * P],
                                                      w_head[:, b, c, :], start=(c == 0 and a == b == HI),
                                                      stop=(c == HK - 1 and a == LO))
                            if c == HK - 1:
                                mm.then_inc(y_acc, 1)


_PREFIX = "L0_rec_"
_OUT = (2048, 512)


def kernel(**inputs):
    import numpy as _np
    import concourse.bacc as _bacc
    from concourse import mybir as _mybir
    from concourse.bass_utils import run_bass_kernel_spmd as _run

    nc = _bacc.Bacc("TRN2", target_bir_lowering=False, num_devices=1)
    arrays, tensors = {}, {}
    for name, value in inputs.items():
        a = _np.ascontiguousarray(value)
        arrays[f"in_{name}"] = a
        tensors[name.replace(_PREFIX, "")] = nc.dram_tensor(f"in_{name}", a.shape, _mybir.dt.from_np(a.dtype),
                                                            kind="ExternalInput").ap()
    tensors["out"] = nc.dram_tensor("out_0", _OUT, _mybir.dt.from_np(_np.dtype("float32")),
                                    kind="ExternalOutput").ap()
    build(nc, tensors)
    return _run(nc, [arrays], core_ids=[0]).results[0]["out_0"]
```
